# Optimizing a Trainium2 kernel written in Bass

```python
import numpy as np
import jax
import jax.numpy as jnp

def _softmax(x, axis=-1):
    return jax.nn.softmax(x, axis=axis)

def _gelu(x):
    return jax.nn.gelu(x, approximate=True)

def _silu(x):
    return jax.nn.silu(x)

def _sigmoid(x):
    return jax.nn.sigmoid(x)

def _layernorm(x, axis=-1, eps=1e-05):
    m = jnp.mean(x, axis=axis, keepdims=True)
    v = jnp.var(x, axis=axis, keepdims=True)
    return (x - m) / jnp.sqrt(v + eps)

def _scatter_add(tgt, idx, src, axis=0):
    return tgt.at[idx].add(src)

def _segment_sum(src, seg, n):
    return jax.ops.segment_sum(src, seg, n)
kernel_name = 'mk_gnn_resnorm_d1_gnn_r8_a0a5e6'

def setup_inputs(seed: int=0):
    np.random.seed(seed)
    _w = jnp.asarray

    def _rec_inputs():
        import jax
        import jax.numpy as jnp
        _gk = jax.random.key(seed)
        x = -0.000202 + 1 * jax.random.normal(jax.random.fold_in(_gk, 1), (6250, 128), jnp.float32)
        _s = jax.random.randint(jax.random.fold_in(_gk, 2), (100000,), 0, 6250, jnp.int32)
        _d = jax.random.randint(jax.random.fold_in(_gk, 3), (100000,), 0, 6250, jnp.int32)
        _loop = jnp.arange(6250, dtype=jnp.int32)
        src = jnp.concatenate([_s, _d, _loop])
        dst = jnp.concatenate([_d, _s, _loop])
        _o = jnp.argsort(dst, stable=True)
        src = src[_o]
        dst = dst[_o]
        return (x, src, dst)
    x, src, dst = _rec_inputs()

    def _L0_gnn_setup():
        import jax, jax.numpy as jnp
        import numpy as np
        N_NODES = 6250
        N_EDGES = 100000
        NODE_DIM = 128
        HIDDEN = 128
        N_LAYERS = 2
        EPS = 1e-05

        def _layer_norm(h, gamma, beta):
            mu = jnp.mean(h, axis=-1, keepdims=True)
            var = jnp.mean(jnp.square(h - mu), axis=-1, keepdims=True)
            return (h - mu) * jax.lax.rsqrt(var + EPS) * gamma + beta
        key = jax.random.key(seed)
        ks = jax.random.split(key, 12)
        s = 0.05
        x = jax.random.normal(ks[0], (N_NODES, NODE_DIM), jnp.float32)
        edge_index = jax.random.randint(ks[1], (2, N_EDGES), 0, N_NODES, dtype=jnp.int64)
        W_enc = jax.random.normal(ks[2], (HIDDEN, NODE_DIM), jnp.float32) * s
        b_enc = jnp.zeros((HIDDEN,), jnp.float32)
        Wm1 = jax.random.normal(ks[3], (N_LAYERS, HIDDEN, 2 * HIDDEN), jnp.float32) * s
        bm1 = jnp.zeros((N_LAYERS, HIDDEN), jnp.float32)
        Wm2 = jax.random.normal(ks[4], (N_LAYERS, HIDDEN, HIDDEN), jnp.float32) * s
        bm2 = jnp.zeros((N_LAYERS, HIDDEN), jnp.float32)
        Wu = jax.random.normal(ks[5], (N_LAYERS, HIDDEN, 2 * HIDDEN), jnp.float32) * s
        bu = jnp.zeros((N_LAYERS, HIDDEN), jnp.float32)
        gamma = jnp.ones((N_LAYERS, HIDDEN), jnp.float32)
        beta = jnp.zeros((N_LAYERS, HIDDEN), jnp.float32)
        W_out = jax.random.normal(ks[6], (HIDDEN, HIDDEN), jnp.float32) * s
        b_out = jnp.zeros((HIDDEN,), jnp.float32)
        return {'x': x, 'edge_index': edge_index, 'W_enc': W_enc, 'b_enc': b_enc, 'Wm1': Wm1, 'bm1': bm1, 'Wm2': Wm2, 'bm2': bm2, 'Wu': Wu, 'bu': bu, 'gamma': gamma, 'beta': beta, 'W_out': W_out, 'b_out': b_out}
    _L0_gnn_all = _L0_gnn_setup()
    _L0_gnn_in = {k: v for k, v in _L0_gnn_all.items() if k in ('W_enc', 'b_enc', 'Wm1', 'bm1', 'Wm2', 'bm2', 'Wu', 'bu', 'gamma', 'beta', 'W_out', 'b_out')}
    del _L0_gnn_all
    return {'x': x, 'src': src, 'dst': dst, 'L0_gnn_W_enc': _L0_gnn_in['W_enc'], 'L0_gnn_b_enc': _L0_gnn_in['b_enc'], 'L0_gnn_Wm1': _L0_gnn_in['Wm1'], 'L0_gnn_bm1': _L0_gnn_in['bm1'], 'L0_gnn_Wm2': _L0_gnn_in['Wm2'], 'L0_gnn_bm2': _L0_gnn_in['bm2'], 'L0_gnn_Wu': _L0_gnn_in['Wu'], 'L0_gnn_bu': _L0_gnn_in['bu'], 'L0_gnn_gamma': _L0_gnn_in['gamma'], 'L0_gnn_beta': _L0_gnn_in['beta'], 'L0_gnn_W_out': _L0_gnn_in['W_out'], 'L0_gnn_b_out': _L0_gnn_in['b_out']}

def reference(x, src, dst, L0_gnn_W_enc, L0_gnn_b_enc, L0_gnn_Wm1, L0_gnn_bm1, L0_gnn_Wm2, L0_gnn_bm2, L0_gnn_Wu, L0_gnn_bu, L0_gnn_gamma, L0_gnn_beta, L0_gnn_W_out, L0_gnn_b_out):
    import jax
    import jax.numpy as jnp

    def _L0_gnn_ref(x, edge_index, W_enc, b_enc, Wm1, bm1, Wm2, bm2, Wu, bu, gamma, beta, W_out, b_out):
        import jax, jax.numpy as jnp
        import numpy as np
        N_NODES = 6250
        N_EDGES = 100000
        NODE_DIM = 128
        HIDDEN = 128
        N_LAYERS = 2
        EPS = 1e-05

        def _layer_norm(h, gamma, beta):
            mu = jnp.mean(h, axis=-1, keepdims=True)
            var = jnp.mean(jnp.square(h - mu), axis=-1, keepdims=True)
            return (h - mu) * jax.lax.rsqrt(var + EPS) * gamma + beta
        row, col = (edge_index[0], edge_index[1])
        h = x @ W_enc.T + b_enc
        for l in range(N_LAYERS):
            m = jnp.concatenate([h[row], h[col]], axis=-1)
            m = jax.nn.relu(m @ Wm1[l].T + bm1[l])
            m = m @ Wm2[l].T + bm2[l]
            agg = jax.ops.segment_sum(m, col, num_segments=N_NODES)
            upd = jnp.concatenate([h, agg], axis=-1) @ Wu[l].T + bu[l]
            h = _layer_norm(h + upd, gamma[l], beta[l])
        return h @ W_out.T + b_out
    edge_index = jnp.stack([src, dst])
    x = _layernorm(x + _L0_gnn_ref(x, edge_index, L0_gnn_W_enc, L0_gnn_b_enc, L0_gnn_Wm1, L0_gnn_bm1, L0_gnn_Wm2, L0_gnn_bm2, L0_gnn_Wu, L0_gnn_bu, L0_gnn_gamma, L0_gnn_beta, L0_gnn_W_out, L0_gnn_b_out), axis=-1)
    return x

_drawn_inputs = setup_inputs


def setup_inputs(seed=0):
    import zlib

    import numpy as np

    out = dict(_drawn_inputs(seed))
    spreads = {'L0_gnn_b_enc': (0.0, 0.1),
     'L0_gnn_bm1': (0.0, 0.1),
     'L0_gnn_bm2': (0.0, 0.1),
     'L0_gnn_bu': (0.0, 0.46),
     'L0_gnn_gamma': (1.0, 0.2),
     'L0_gnn_beta': (0.0, 0.1),
     'L0_gnn_b_out': (0.0, 0.1)}
    factors = {}
    for name, (base, spread) in spreads.items():
        noise = np.random.default_rng([zlib.crc32(name.encode()), seed]).standard_normal(out[name].shape)
        drawn = base * np.exp(spread * noise) if base else spread * noise
        out[name] = jnp.asarray(drawn.astype(out[name].dtype))
    for name, factor in factors.items():
        out[name] = (out[name] * factor).astype(out[name].dtype)
    return out
```

```python
import numpy as np

FEAT = 128
TILE = 128
TPG = 4
GROUP = TILE * TPG
WIN = 128
CHUNK = 512
SUB = CHUNK // 128
SLOTS = 8
HALF = SLOTS // 2
LAYERS = 2
EPS = 1e-5
NO_NODE = 1 << 20


def sizes(nodes, edges):
    groups = -(-edges // GROUP)
    chunks = -(-nodes // CHUNK)
    per_row = -(-groups // 128)
    return groups, chunks, chunks * CHUNK, per_row, -(-nodes // WIN)


def build(nc, d, nodes, edges):
    import concourse.bass as bass
    from concourse import mybir
    from contextlib import ExitStack

    fp32, bf16, i32 = mybir.dt.float32, mybir.dt.bfloat16, mybir.dt.int32
    ALU, ACT = mybir.AluOpType, mybir.ActivationFunctionType
    AX = mybir.AxisListType
    GROUPS, CHUNKS, NPAD, PER_ROW, WINDOWS = sizes(nodes, edges)
    PARTS = 3
    TOP = NPAD - WIN

    ctx = ExitStack()
    with ctx:
        def sb(name, shape, dt=fp32):
            return ctx.enter_context(nc.sbuf_tensor(name, shape, dt))

        def sem(name):
            return ctx.enter_context(nc.semaphore(name))

        a_table = nc.dram_tensor("a_table", (NPAD, FEAT), fp32, kind="Internal").ap()
        b_table = nc.dram_tensor("b_table", (NPAD, PARTS * FEAT), bf16, kind="Internal").ap()
        base_dram = nc.dram_tensor("base_dram", (128, PER_ROW), fp32, kind="Internal").ap()

        xT = sb("xT", [FEAT, NPAD])
        hT = sb("hT", [FEAT, NPAD])
        acc = sb("acc", [FEAT, NPAD])
        degree = sb("degree", [1, NPAD])
        dst_i = sb("dst_i", [TILE, GROUPS * TPG], i32)
        dst_f = sb("dst_f", [TILE, GROUPS * TPG])
        rel = sb("rel", [TILE, GROUPS * TPG])
        base_all = sb("base_all", [128, 128 * PER_ROW])
        base_row = sb("base_row", [1, 128 * PER_ROW], i32)
        w_enc = sb("w_enc", [FEAT, FEAT])
        w_out = sb("w_out", [FEAT, FEAT])
        w_m1 = sb("w_m1", [FEAT, LAYERS, 2 * FEAT])
        w_m2 = sb("w_m2", [FEAT, LAYERS, FEAT])
        w_uh = sb("w_uh", [FEAT, LAYERS, FEAT])
        w_ua = sb("w_ua", [FEAT, LAYERS, FEAT])
        cols = sb("cols", [FEAT, 2 + 3 * LAYERS])
        bm2_row = sb("bm2_row", [1, LAYERS, FEAT])
        bm1_all = sb("bm1_all", [128, LAYERS, FEAT])
        iota_i = sb("iota_i", [128, 128], i32)
        part_i = sb("part_i", [128, 1], i32)
        win_i = sb("win_i", [128, WINDOWS], i32)
        iota = sb("iota", [128, 128])
        part = sb("part", [128, 1])
        win_start = sb("win_start", [128, WINDOWS])
        ident = sb("ident", [128, 128])
        ones_col = sb("ones_col", [128, 1])
        averager = sb("averager", [128, 128])
        eps_col = sb("eps_col", [128, 1])
        gmin = sb("gmin", [128, PER_ROW])
        gmax = sb("gmax", [128, PER_ROW])
        base = sb("base", [128, PER_ROW])
        wide = sb("wide", [128, PER_ROW])
        wide_any = sb("wide_any", [128, 1])
        flag = sb("flag", [1, 1], i32)
        src_ix = sb("src_ix", [TILE, SLOTS, TPG], i32)
        rows = sb("rows", [TILE, SLOTS, GROUP])
        window = sb("window", [WIN, SLOTS, PARTS * FEAT], bf16)
        onehot = sb("onehot", [TILE, 2, GROUP])
        spread = sb("spread", [WIN, 2, GROUP], bf16)
        pre = sb("pre", [TILE, 2, GROUP])
        msg = sb("msg", [TILE, 2, GROUP])
        rel_win = sb("rel_win", [TILE, TPG])
        h_new = rows[:, 0:2, :]
        a_stage = rows[:, 2:4, :]
        b_full = rows[:, 4, :]
        b_rest = rows[:, 5, :]
        sq = rows[:, 6, :]
        std = rows[:, 7, :]
        b_stage = sb("b_stage", [128, 2, SUB, PARTS, FEAT], bf16)
        agg_s = onehot[:, 0, :]
        u_s = onehot[:, 1, :]
        dev = pre[:, 0, :]
        rstd = pre[:, 1, :]
        y_out = msg
        RUN = PER_ROW * GROUP
        dst_g = acc[:, 0:RUN].bitcast(i32)
        dst_gf = acc[:, RUN:2 * RUN]
        dst_gv = acc[:, 2 * RUN:3 * RUN]
        assert 3 * RUN <= NPAD

        ps = ctx.enter_context(nc.psum_tensor("ps", [128, 8, 512], fp32))
        flipped, picked, summed_ps = ps[:, 0:2, :], ps[:, 2:4, :], ps[:, 4:6, :]
        agg_ps, upd_ps, mean_ps, var_ps = (ps[:, k, :] for k in range(4))
        a_ps, b_ps = ([ps[:, 4 + 2 * q + k, :].rearrange("p (k f) -> p k f", k=SUB) for q in range(2)] for k in range(2))

        inputs_in = sem("inputs_in")
        x_in = sem("x_in")
        dst_in = sem("dst_in")
        iotas_made = sem("iotas_made")
        consts_made = sem("consts_made")
        dve_step = sem("dve_step")
        wide_found = sem("wide_found")
        wide_counted = sem("wide_counted")
        flag_ready = sem("flag_ready")
        base_found = sem("base_found")
        base_stored = sem("base_stored")
        base_spread = sem("base_spread")
        rows_of_base = sem("rows_of_base")
        rel_ready = sem("rel_ready")
        enc_ready = sem("enc_ready")
        agg_ready = sem("agg_ready")
        agg_copied = sem("agg_copied")
        upd_ready = sem("upd_ready")
        u_ready = sem("u_ready")
        mean_ready = sem("mean_ready")
        dev_ready = sem("dev_ready")
        sq_ready = sem("sq_ready")
        var_ready = sem("var_ready")
        std_ready = sem("std_ready")
        rstd_ready = sem("rstd_ready")
        norm_ready = sem("norm_ready")
        h_ready = sem("h_ready")
        h_kept = sem("h_kept")
        table_ready = sem("table_ready")
        a_staged = sem("a_staged")
        b_full_ready = sem("b_full_ready")
        b_hi_ready = sem("b_hi_ready")
        b_rest_ready = sem("b_rest_ready")
        b_mid_ready = sem("b_mid_ready")
        b_staged = sem("b_staged")
        a_stored = [sem(f"a_stored{q}") for q in range(2)]
        b_stored = [sem(f"b_stored{q}") for q in range(2)]
        tables_stored = sem("tables_stored")
        proj_ready = sem("proj_ready")
        out_ready = sem("out_ready")
        y_stored = [sem(f"y_stored{q}") for q in range(2)]
        out_stored = sem("out_stored")
        acc_clear = sem("acc_clear")
        src_ready = [sem(f"src_ready{k}") for k in range(2)]
        rows_ready = [sem(f"rows_ready{k}") for k in range(SLOTS)]
        window_ready = [sem(f"window_ready{k}") for k in range(SLOTS)]
        onehot_ready = sem("onehot_ready")
        flipped_ready = sem("flipped_ready")
        spread_ready = sem("spread_ready")
        picked_ready = sem("picked_ready")
        pre_ready = sem("pre_ready")
        msg_ready = sem("msg_ready")
        summed_ready = sem("summed_ready")
        added = sem("added")
        edges_done = sem("edges_done")
        g_src_ready = sem("g_src_ready")
        g_rows_ready = sem("g_rows_ready")
        g_window_ready = sem("g_window_ready")
        g_rel_ready = sem("g_rel_ready")
        g_onehot_ready = sem("g_onehot_ready")
        g_flipped_ready = sem("g_flipped_ready")
        g_spread_ready = sem("g_spread_ready")
        g_picked_ready = sem("g_picked_ready")
        g_pre_ready = sem("g_pre_ready")
        g_msg_ready = sem("g_msg_ready")
        g_summed_ready = sem("g_summed_ready")
        g_added = sem("g_added")

        WEIGHTS = ("w_enc", "w_out", "w_m1", "w_m2", "w_uh", "w_ua", "cols", "bm2_row")
        LOADS = 16 * (len(WEIGHTS) + 1)

        block = ctx.enter_context(nc.Block())

        def in_chunks(eng, body):
            if CHUNKS >= 2:
                with eng.Fori(0, CHUNKS // 2) as i:
                    for q in range(2):
                        body(i * 2 + q, q)
            if CHUNKS % 2:
                body(CHUNKS - 1, 0)

        def in_groups(eng, body):
            full = (GROUPS - 1) // SLOTS
            if full:
                with eng.Fori(0, full) as b:
                    body(b, range(SLOTS))
            body(full, range(GROUPS - full * SLOTS))

        def is_last(b, s):
            return isinstance(b, int) and b * SLOTS + s == GROUPS - 1

        def rounds(layer, slot):
            return layer * (-(-(GROUPS - slot) // SLOTS))

        def load_starts(engine, b, n):
            _, starts = nc.values_load_multi_w_load_instructions(
                base_row[0:1, bass.ds(b * SLOTS, n)], engines=[engine], min_val=0, max_val=TOP,
                skip_runtime_bounds_check_because="the starts were clamped to 0..TOP where they were found")
            return starts

        def chunk(buf, c):
            return buf[:, bass.ds(c * CHUNK, CHUNK)]

        def stored(stage, q):
            return stage * ((CHUNKS + 1 - q) // 2)

        def norm_count(stage, c, again):
            return c if stage == 1 else CHUNKS + c * 2 + again

        @block.sync
        def _(sp):
            sp.dma_start(dst_g, d["dst_groups"]).then_inc(dst_in, 16)
            sp.dma_start(dst_i[:, :], d["dst_tiles"]).then_inc(dst_in, 16)
            sp.dma_start(xT[:, :], d["xT"]).then_inc(x_in, 16)
            for name, buf in zip(WEIGHTS, (w_enc, w_out, w_m1, w_m2, w_uh, w_ua, cols, bm2_row)):
                view = buf[:, :, :] if len(buf.shape) == 3 else buf[:, :]
                sp.dma_start(view, d[name]).then_inc(inputs_in, 16)
            sp.dma_start(bm1_all[:, :, :], d["bm1"].rearrange("(o l) f -> o l f", o=1).broadcast_to([128, LAYERS, FEAT])
                         ).then_inc(inputs_in, 16)
            sp.wait_ge(base_found, 1)
            sp.dma_start(base_dram, base[:, :]).then_inc(base_stored, 16)
            sp.wait_ge(base_stored, 16)
            sp.dma_start(base_all[:, :], base_dram.rearrange("(o p) k -> o (p k)", o=1).broadcast_to([128, 128 * PER_ROW])
                         ).then_inc(base_spread, 16)

            def store_tables(stage):
                def body(c, q):
                    n = c + stage * CHUNKS
                    to = bass.ds(c * CHUNK, CHUNK)
                    sp.wait_ge(a_staged, n + 1)
                    sp.dma_start(a_table[to, :].rearrange("(k p) f -> p k f", p=128),
                                 a_stage[:, q, :].rearrange("p (k f) -> p k f", k=SUB)).then_inc(a_stored[q], 16)
                    sp.wait_ge(b_staged, n + 1 + 2)
                    sp.dma_start(b_table[to, :].rearrange("(k p) f -> p k f", p=128),
                                 b_stage[:, q, :, :, :].rearrange("p k t f -> p k (t f)")).then_inc(b_stored[q], 16)
                    used = (c - q) // 2 + 1 + stored(stage, q)
                    sp.wait_ge(a_stored[q], used * 16)
                    sp.wait_ge(b_stored[q], used * 16)
                    sp.sem_inc(tables_stored, 1)
                in_chunks(sp, body)

            def few_windows(layer):
                def body(b, slots):
                    starts = load_starts(mybir.EngineType.SP, b, len(slots))
                    for s in slots:
                        g = b * SLOTS + s + layer * GROUPS
                        if s % HALF == 0:
                            k = s // HALF
                            at = b * (SLOTS * TPG) + s * TPG
                            n_ix = min(HALF, len(slots) - s) * TPG
                            sp.wait_ge(pre_ready, g + n_ix // TPG)
                            sp.dma_start(src_ix[:, s:s + n_ix // TPG, :].rearrange("p s t -> p (s t)"),
                                         d["src_tiles"][:, bass.ds(at, n_ix)]).then_inc(src_ready[k], 16)
                        sp.wait_ge(picked_ready, g + 1)
                        sp.dma_start(window[:, s, :], b_table[bass.ds(starts[s], WIN), :]).then_inc(window_ready[s], 16)
                in_groups(sp, body)

            def all_windows(layer):
                with sp.Fori(0, GROUPS) as g:
                    n = g + layer * GROUPS
                    sp.wait_ge(g_added, n * WINDOWS + 1)
                    sp.dma_start(src_ix[:, 0, :], d["src_tiles"][:, bass.ds(g * TPG, TPG)]).then_inc(g_src_ready, 16)
                    with sp.Fori(0, WINDOWS) as w:
                        sp.wait_ge(g_added, n * WINDOWS + w + 1)
                        sp.dma_start(window[:, 0, :], b_table[bass.ds(w * WIN, WIN), :]).then_inc(g_window_ready, 16)

            sp.wait_ge(flag_ready, 1)
            many = sp.value_load(flag[0:1, 0:1], min_val=0, max_val=1)
            sp.wait_ge(rows_of_base, 1)
            for layer in range(LAYERS):
                store_tables(layer)
                with sp.If(many == 0):
                    few_windows(layer)
                with sp.Else():
                    all_windows(layer)

            def store_out(c, q):
                sp.wait_ge(out_ready, c + 1)
                sp.dma_start(d["yT"][:, bass.ds(c * CHUNK, CHUNK)], y_out[:, q, :]).then_inc(y_stored[q], 16)
                sp.wait_ge(y_stored[q], ((c - q) // 2 + 1) * 16)
                sp.sem_inc(out_stored, 1)
            in_chunks(sp, store_out)

        @block.gpsimd
        def _(pool):
            pool.iota(iota_i[:, :], pattern=[[1, 128]], base=0, channel_multiplier=0).then_inc(iotas_made, 1)
            pool.iota(part_i[:, :], pattern=[[0, 1]], base=0, channel_multiplier=1).then_inc(iotas_made, 1)
            pool.iota(win_i[:, :], pattern=[[WIN, WINDOWS]], base=0, channel_multiplier=0).then_inc(iotas_made, 1)
            pool.wait_ge(flag_ready, 1)
            many = pool.value_load(flag[0:1, 0:1], min_val=0, max_val=1)

            def gather(slot, t, done):
                pool.indirect_dma_start(
                    out=rows[:, slot, t * FEAT:(t + 1) * FEAT], out_offset=None, in_=a_table[:, :],
                    in_offset=bass.IndirectOffsetOnAxis(ap=src_ix[:, slot, t:t + 1], axis=0)).then_inc(done, 16)

            def few_windows(layer):
                def body(b, slots):
                    for s in slots:
                        if s % HALF == 0:
                            k = s // HALF
                            pool.wait_ge(src_ready[k], (b + 1) * 16 + 16 * rounds(layer, s))
                            pool.nop(nofuse=True)
                        pool.wait_ge(pre_ready, b * SLOTS + s + layer * GROUPS + 1)
                        pool.nop(nofuse=True)
                        for t in range(TPG):
                            gather(s, t, rows_ready[s])
                in_groups(pool, body)

            def all_windows(layer):
                with pool.Fori(0, GROUPS) as g:
                    pool.wait_ge(g_src_ready, (g + layer * GROUPS + 1) * 16)
                    pool.nop(nofuse=True)
                    for t in range(TPG):
                        gather(0, t, g_rows_ready)

            for layer in range(LAYERS):
                pool.wait_ge(tables_stored, (layer + 1) * CHUNKS + 2)
                pool.wait_ge(h_kept, (layer + 1) * CHUNKS)
                pool.nop(nofuse=True)
                with pool.If(many == 0):
                    few_windows(layer)
                with pool.Else():
                    all_windows(layer)

        @block.tensor
        def _(pe):
            pe.wait_ge(consts_made, 1)
            pe.wait_ge(wide_found, 1)
            nc.tensor.matmul(ps[0:1, 7, 0:1], wide_any[:, :], ones_col[:, :], start=True, stop=True).then_inc(wide_counted, 1)
            pe.wait_ge(inputs_in, LOADS)
            pe.wait_ge(x_in, 16)
            pe.wait_ge(flag_ready, 1)
            many = pe.value_load(flag[0:1, 0:1], min_val=0, max_val=1)

            def tables(stage, c, q):
                n = c + stage * CHUNKS
                pe.wait_ge(h_ready, n + 2)
                pe.wait_ge(b_staged, n + 1)
                for out, of in ((a_ps[q], 0), (b_ps[q], FEAT)):
                    for k in range(SUB):
                        last = nc.tensor.matmul(out[:, k, :], h_new[:, q, k * 128:(k + 1) * 128],
                                                w_m1[:, stage, of:of + FEAT], start=True, stop=True)
                last.then_inc(table_ready, 1)

            def encode(c, q):
                pe.wait_ge(h_ready, c + 1)
                nc.tensor.matmul(upd_ps, w_enc[:, :], chunk(xT, c), start=True, stop=True).then_inc(enc_ready, 1)

            def norm(m):
                pe.wait_ge(u_ready, m + 1)
                nc.tensor.matmul(mean_ps, averager[:, :], u_s, start=True, stop=True).then_inc(mean_ready, 1)
                pe.wait_ge(sq_ready, m + 1)
                nc.tensor.matmul(var_ps, averager[:, :], sq, start=True, stop=True).then_inc(var_ready, 1)

            def update(stage, c, q):
                layer = stage - 1
                n = c + layer * CHUNKS
                nc.tensor.matmul(agg_ps, w_m2[:, layer, :], chunk(acc, c), start=True, stop=False)
                nc.tensor.matmul(agg_ps, bm2_row[:, layer, :], chunk(degree, c), start=False, stop=True
                                 ).then_inc(agg_ready, 1)
                nc.tensor.matmul(upd_ps, w_uh[:, layer, :], chunk(hT, c), start=True, stop=False)
                pe.wait_ge(agg_copied, n + 1)
                nc.tensor.matmul(upd_ps, w_ua[:, layer, :], agg_s, start=False, stop=True).then_inc(upd_ready, 1)
                norm(norm_count(stage, c, 0))

            def flip(q, done):
                for t in range(TPG):
                    at = slice(t * 128, (t + 1) * 128)
                    last = nc.tensor.transpose(flipped[:, q, at], onehot[:, q, at], ident[:, :])
                last.then_inc(done, 1)

            def pick(s, q, done):
                for t in range(TPG):
                    at = slice(t * 128, (t + 1) * 128)
                    for part_ in range(PARTS):
                        last = nc.tensor.matmul(picked[:, q, at], spread[:, q, at],
                                                window[:, s, part_ * FEAT:(part_ + 1) * FEAT],
                                                start=(part_ == 0), stop=(part_ == PARTS - 1))
                last.then_inc(done, 1)

            def sum_up(layer, q, done):
                for t in range(TPG):
                    at = slice(t * 128, (t + 1) * 128)
                    last = nc.tensor.matmul(summed_ps[:, q, 0:WIN], msg[:, q, at], onehot[:, q, at],
                                            start=(t == 0), stop=(t == TPG - 1))
                if layer == 0:
                    for t in range(TPG):
                        at = slice(t * 128, (t + 1) * 128)
                        last = nc.tensor.matmul(summed_ps[0:1, q, WIN:2 * WIN], ones_col[:, :], onehot[:, q, at],
                                                start=(t == 0), stop=(t == TPG - 1))
                last.then_inc(done, 1)

            def few_windows(layer):
                def flip_group(g, q):
                    pe.wait_ge(onehot_ready, g + SLOTS + 1)
                    pe.wait_ge(spread_ready, g + SLOTS - 1)
                    flip(q, flipped_ready)

                def body(b, slots):
                    for s in slots:
                        g, q = b * SLOTS + s + layer * GROUPS, s % 2
                        pe.wait_ge(spread_ready, g + SLOTS + 1)
                        pe.wait_ge(window_ready[s], (b + 1) * 16 + 16 * rounds(layer, s))
                        pe.wait_ge(pre_ready, g + SLOTS - 1)
                        pick(s, q, picked_ready)
                        if not is_last(b, s):
                            flip_group(g + 1, 1 - q)
                        pe.wait_ge(msg_ready, g + SLOTS + 1)
                        pe.wait_ge(added, g + SLOTS - 1)
                        sum_up(layer, q, summed_ready)
                flip_group(layer * GROUPS, 0)
                in_groups(pe, body)

            def all_windows(layer):
                with pe.Fori(0, GROUPS) as g:
                    with pe.Fori(0, WINDOWS) as w:
                        n = (g + layer * GROUPS) * WINDOWS + w
                        pe.wait_ge(g_onehot_ready, n + 1)
                        flip(0, g_flipped_ready)
                        pe.wait_ge(g_spread_ready, n + 1)
                        pe.wait_ge(g_window_ready, n * 16 + 16)
                        pick(0, 0, g_picked_ready)
                        pe.wait_ge(g_msg_ready, n + 1)
                        sum_up(layer, 0, g_summed_ready)

            def stage0(c, q):
                encode(c, q)
                tables(0, c, q)
            in_chunks(pe, stage0)
            for layer in range(LAYERS):
                pe.wait_ge(b_staged, (layer + 1) * CHUNKS + 2)
                with pe.If(many == 0):
                    few_windows(layer)
                with pe.Else():
                    all_windows(layer)
                pe.wait_ge(edges_done, layer + 1)

                def stage(c, q):
                    update(layer + 1, c, q)
                    if layer + 1 < LAYERS:
                        tables(layer + 1, c, q)
                    else:
                        pe.wait_ge(h_ready, c + LAYERS * CHUNKS + 2)
                        nc.tensor.matmul(agg_ps, w_out[:, :], h_new[:, q, :], start=True, stop=True).then_inc(proj_ready, 1)
                        norm(norm_count(layer + 1, c, 1))
                in_chunks(pe, stage)

        @block.scalar
        def _(act):
            act.wait_ge(inputs_in, LOADS)
            act.wait_ge(flag_ready, 1)
            many = act.value_load(flag[0:1, 0:1], min_val=0, max_val=1)

            def tables(stage, c, q):
                n = c + stage * CHUNKS
                act.wait_ge(table_ready, n + 1)
                act.wait_ge(tables_stored, n + 1)
                nc.scalar.activation(a_stage[:, q, :].rearrange("p (k f) -> p k f", k=SUB),
                                     a_ps[q], ACT.Copy).then_inc(a_staged, 1)

                act.wait_ge(b_full_ready, n + 1)
                nc.scalar.activation(b_stage[:, q, :, 0, :], b_full.rearrange("p (k f) -> p k f", k=SUB),
                                     ACT.Copy).then_inc(b_hi_ready, 1)
                act.wait_ge(b_rest_ready, n + 1)
                nc.scalar.activation(b_stage[:, q, :, 1, :], b_rest.rearrange("p (k f) -> p k f", k=SUB),
                                     ACT.Copy).then_inc(b_mid_ready, 1)

            def norm(m):
                act.wait_ge(dev_ready, m + 1)
                nc.scalar.activation(sq, dev, ACT.Square).then_inc(sq_ready, 1)
                act.wait_ge(var_ready, m + 1)
                nc.scalar.activation(std, var_ps, ACT.Sqrt, bias=eps_col[:, :]).then_inc(std_ready, 1)

            def keep(stage, c, q):
                act.wait_ge(h_ready, c + stage * CHUNKS + 1 + 1)
                nc.scalar.activation(chunk(hT, c), h_new[:, q, :], ACT.Copy).then_inc(h_kept, 1)

            def few_windows(layer):
                def spread_group(g, q):
                    act.wait_ge(flipped_ready, g + SLOTS + 1)
                    act.wait_ge(picked_ready, g + SLOTS - 1)
                    nc.scalar.activation(spread[:, q, :], flipped[:, q, :], ACT.Copy).then_inc(spread_ready, 1)

                def body(b, slots):
                    for s in slots:
                        g, q = b * SLOTS + s + layer * GROUPS, s % 2
                        act.wait_ge(pre_ready, g + SLOTS + 1)
                        act.wait_ge(summed_ready, g + SLOTS - 1)
                        nc.scalar.activation(msg[:, q, :], pre[:, q, :], ACT.Relu).then_inc(msg_ready, 1)
                        if not is_last(b, s):
                            spread_group(g + 1, 1 - q)
                spread_group(layer * GROUPS, 0)
                in_groups(act, body)

            def all_windows(layer):
                with act.Fori(0, GROUPS) as g:
                    with act.Fori(0, WINDOWS) as w:
                        n = (g + layer * GROUPS) * WINDOWS + w
                        act.wait_ge(g_flipped_ready, n + 1)
                        nc.scalar.activation(spread[:, 0, :], flipped[:, 0, :], ACT.Copy).then_inc(g_spread_ready, 1)
                        act.wait_ge(g_pre_ready, n + 1)
                        nc.scalar.activation(msg[:, 0, :], pre[:, 0, :], ACT.Relu).then_inc(g_msg_ready, 1)

            def stage0(c, q):
                act.wait_ge(enc_ready, c + 1)
                nc.scalar.activation(h_new[:, q, :], upd_ps, ACT.Identity, bias=cols[:, 0:1]).then_inc(h_ready, 1)
                keep(0, c, q)
                tables(0, c, q)
            in_chunks(act, stage0)
            for layer in range(LAYERS):
                with act.If(many == 0):
                    few_windows(layer)
                with act.Else():
                    all_windows(layer)

                def stage(c, q):
                    n = c + layer * CHUNKS
                    act.wait_ge(agg_ready, n + 1)
                    nc.scalar.activation(agg_s, agg_ps, ACT.Copy).then_inc(agg_copied, 1)
                    norm(norm_count(layer + 1, c, 0))
                    if layer + 1 < LAYERS:
                        keep(layer + 1, c, q)
                        tables(layer + 1, c, q)
                    else:
                        norm(norm_count(layer + 1, c, 1))
                in_chunks(act, stage)

        @block.vector
        def _(dve):
            steps = [0]

            def link(ins):
                steps[0] += 1
                ins.then_inc(dve_step, 1)
                dve.wait_ge(dve_step, steps[0])

            for ring in (onehot_ready, flipped_ready, spread_ready, picked_ready, pre_ready, msg_ready,
                         summed_ready, added):
                dve.sem_inc(ring, SLOTS)
            dve.sem_inc(h_ready, 1)
            for ring in (b_staged, tables_stored, out_stored):
                dve.sem_inc(ring, 2)
            dve.sem_inc(g_added, 1)

            nc.vector.memset(ones_col[:, :], 1.0)
            nc.vector.memset(averager[:, :], 1.0 / FEAT)
            nc.vector.memset(eps_col[:, :], EPS)
            nc.vector.memset(degree[:, :], 0.0)
            dve.wait_ge(iotas_made, 3)
            nc.vector.tensor_copy(iota[:, :], iota_i[:, :])
            nc.vector.tensor_copy(win_start[:, :], win_i[:, :])
            link(nc.vector.tensor_copy(part[:, :], part_i[:, :]))
            nc.vector.tensor_scalar(ident[:, :], iota[:, :], part[:, 0:1], None, ALU.is_equal).then_inc(consts_made, 1)

            dve.wait_ge(dst_in, 32)
            link(nc.vector.tensor_copy(dst_gf, dst_g))
            by_group = dst_gf.rearrange("p (k e) -> p k e", e=GROUP)
            nc.vector.tensor_reduce(gmin[:, :], by_group, AX.X, ALU.min)
            link(nc.vector.scalar_tensor_tensor(dst_gv, dst_gf, float(NO_NODE), dst_gf, ALU.is_lt, ALU.mult))
            nc.vector.tensor_reduce(gmax[:, :], dst_gv.rearrange("p (k e) -> p k e", e=GROUP), AX.X, ALU.max)
            link(nc.vector.tensor_scalar(base[:, :], gmin[:, :], float(TOP), 0.0, ALU.min, ALU.max))
            base_found_ = nc.vector.tensor_tensor(gmin[:, :], gmax[:, :], base[:, :], ALU.subtract)
            base_found_.then_inc(base_found, 1)
            dve.wait_ge(base_found, 1)
            link(nc.vector.tensor_scalar(wide[:, :], gmin[:, :], float(WIN), None, ALU.is_ge))
            nc.vector.tensor_reduce(wide_any[:, :], wide[:, :], AX.X, ALU.max).then_inc(wide_found, 1)
            dve.wait_ge(wide_counted, 1)
            nc.vector.tensor_scalar(flag[:, :], ps[0:1, 7, 0:1], 0.0, None, ALU.is_gt).then_inc(flag_ready, 1)
            dve.wait_ge(flag_ready, 1)
            many = dve.value_load(flag[0:1, 0:1], min_val=0, max_val=1)
            dve.wait_ge(base_spread, 16)
            nc.vector.tensor_copy(base_row[:, :], base_all[0:1, :]).then_inc(rows_of_base, 1)
            dve.wait_ge(rows_of_base, 1)
            link(nc.vector.tensor_copy(dst_f[:, :], dst_i[:, :]))
            nc.vector.tensor_tensor(rel[:, :].rearrange("p (g t) -> p g t", t=TPG),
                                    dst_f[:, :].rearrange("p (g t) -> p g t", t=TPG),
                                    base_all[:, 0:GROUPS].rearrange("p (g o) -> p g o", o=1).broadcast_to([128, GROUPS, TPG]),
                                    ALU.subtract).then_inc(rel_ready, 1)
            dve.wait_ge(rel_ready, 1)
            dve.wait_ge(inputs_in, LOADS)

            def tables(stage, c, q):
                n = c + stage * CHUNKS
                four = lambda buf: buf.rearrange("p (k f) -> p k f", k=SUB)
                dve.wait_ge(table_ready, n + 1)
                nc.vector.tensor_tensor(four(b_full), b_ps[q],
                                        bm1_all[:, stage:stage + 1, :].broadcast_to([128, SUB, FEAT]),
                                        ALU.add).then_inc(b_full_ready, 1)
                dve.wait_ge(b_hi_ready, n + 1)
                nc.vector.tensor_tensor(four(b_rest), four(b_full), b_stage[:, q, :, 0, :],
                                        ALU.subtract).then_inc(b_rest_ready, 1)
                dve.wait_ge(b_mid_ready, n + 1)
                nc.vector.tensor_tensor(b_stage[:, q, :, 2, :], four(b_rest), b_stage[:, q, :, 1, :],
                                        ALU.subtract).then_inc(b_staged, 1)

            def norm(m):
                dve.wait_ge(mean_ready, m + 1)
                nc.vector.tensor_tensor(dev, u_s, mean_ps, ALU.subtract).then_inc(dev_ready, 1)
                dve.wait_ge(std_ready, m + 1)
                nc.vector.reciprocal(rstd, std).then_inc(rstd_ready, 1)
                dve.wait_ge(rstd_ready, m + 1)

            def one_hots(rel_cols, q):
                return nc.vector.tensor_tensor(
                    onehot[:, q, :].rearrange("p (t n) -> p t n", t=TPG),
                    iota[:, :].rearrange("p (o n) -> p o n", o=1).broadcast_to([TILE, TPG, WIN]),
                    rel_cols.rearrange("p (t o) -> p t o", o=1).broadcast_to([TILE, TPG, WIN]), ALU.is_equal)

            def add_sums(layer, start, q, done):
                at = bass.ds(start, WIN)
                last = nc.vector.tensor_tensor(acc[:, at], acc[:, at], summed_ps[:, q, 0:WIN], ALU.add)
                if layer == 0:
                    last = nc.vector.tensor_tensor(degree[:, at], degree[:, at], summed_ps[0:1, q, WIN:2 * WIN], ALU.add)
                last.then_inc(done, 1)

            def few_windows(layer):
                def onehot_group(g_in_layer, q):
                    g = g_in_layer + layer * GROUPS
                    dve.wait_ge(summed_ready, g + SLOTS - 1)
                    one_hots(rel[:, bass.ds(g_in_layer * TPG, TPG)], q).then_inc(onehot_ready, 1)

                def body(b, slots):
                    starts = load_starts(mybir.EngineType.DVE, b, len(slots))
                    for s in slots:
                        g, q = b * SLOTS + s + layer * GROUPS, s % 2
                        if not is_last(b, s):
                            onehot_group(b * SLOTS + s + 1, 1 - q)
                        dve.wait_ge(rows_ready[s], (b + 1) * (16 * TPG) + 16 * TPG * rounds(layer, s))
                        dve.wait_ge(picked_ready, g + SLOTS + 1)
                        dve.wait_ge(msg_ready, g + SLOTS - 1)
                        nc.vector.tensor_tensor(pre[:, q, :], rows[:, s, :], picked[:, q, :], ALU.add
                                                ).then_inc(pre_ready, 1)
                        dve.wait_ge(summed_ready, g + SLOTS + 1)
                        dve.wait_ge(added, g + SLOTS)
                        add_sums(layer, starts[s], q, added)
                onehot_group(0, 0)
                in_groups(dve, body)
                dve.wait_ge(added, (layer + 1) * GROUPS + SLOTS)

            def all_windows(layer):
                with dve.Fori(0, GROUPS) as g:
                    with dve.Fori(0, WINDOWS) as w:
                        n = (g + layer * GROUPS) * WINDOWS + w
                        nc.vector.tensor_scalar(rel_win[:, :], dst_f[:, bass.ds(g * TPG, TPG)],
                                                win_start[:, bass.ds(w, 1)], None, ALU.subtract).then_inc(g_rel_ready, 1)
                        dve.wait_ge(g_rel_ready, n + 1)
                        one_hots(rel_win[:, :], 0).then_inc(g_onehot_ready, 1)
                        dve.wait_ge(g_rows_ready, (g + layer * GROUPS + 1) * (16 * TPG))
                        dve.wait_ge(g_picked_ready, n + 1)
                        nc.vector.tensor_tensor(pre[:, 0, :], rows[:, 0, :], picked[:, 0, :], ALU.add
                                                ).then_inc(g_pre_ready, 1)
                        dve.wait_ge(g_summed_ready, n + 1)
                        add_sums(layer, w * WIN, 0, g_added)
                        dve.wait_ge(g_added, n + 2)

            def tables_stage0(c, q):
                tables(0, c, q)
            in_chunks(dve, tables_stage0)
            for layer in range(LAYERS):
                nc.vector.memset(acc[:, :], 0.0).then_inc(acc_clear, 1)
                dve.wait_ge(acc_clear, layer + 1)
                with dve.If(many == 0):
                    few_windows(layer)
                with dve.Else():
                    all_windows(layer)
                dve.sem_inc(edges_done, 1)

                def stage(c, q):
                    n = c + layer * CHUNKS
                    bu, gamma, beta = (cols[:, 2 + 3 * layer + k:3 + 3 * layer + k] for k in range(3))
                    dve.wait_ge(upd_ready, n + 1)
                    nc.vector.scalar_tensor_tensor(u_s, upd_ps, bu, chunk(hT, c), ALU.add, ALU.add).then_inc(u_ready, 1)
                    norm(norm_count(layer + 1, c, 0))
                    nc.vector.tensor_tensor(rstd, rstd, dev, ALU.mult).then_inc(norm_ready, 1)
                    dve.wait_ge(norm_ready, n + 1)
                    nc.vector.tensor_scalar(h_new[:, q, :], rstd, gamma, beta, ALU.mult, ALU.add).then_inc(h_ready, 1)
                    if layer + 1 < LAYERS:
                        tables(layer + 1, c, q)
                    else:
                        dve.wait_ge(proj_ready, c + 1)
                        nc.vector.scalar_tensor_tensor(u_s, agg_ps, cols[:, 1:2], chunk(xT, c), ALU.add, ALU.add
                                                       ).then_inc(u_ready, 1)
                        norm(norm_count(layer + 1, c, 1))
                        dve.wait_ge(out_stored, c + 1)
                        nc.vector.tensor_tensor(y_out[:, q, :], rstd, dev, ALU.mult).then_inc(out_ready, 1)
                in_chunks(dve, stage)


def kernel(**inputs):
    import numpy as _np
    import concourse.bacc as _bacc
    from concourse import mybir as _mybir
    from concourse.bass_utils import run_bass_kernel_spmd as _run

    a = {k.removeprefix("L0_gnn_"): _np.asarray(v) for k, v in inputs.items()}
    nodes, edges = a["x"].shape[0], a["src"].shape[0]
    groups, chunks, npad, per_row, _ = sizes(nodes, edges)

    def turned(w):
        return _np.ascontiguousarray(_np.swapaxes(w, -1, -2))

    def by_input(w):
        return _np.ascontiguousarray(_np.swapaxes(w, 0, 1))

    xT = _np.zeros((FEAT, npad), a["x"].dtype)
    xT[:, :nodes] = a["x"].T
    src = _np.zeros(groups * GROUP, a["src"].dtype)
    src[:edges] = a["src"]
    dst = _np.full(128 * per_row * GROUP, NO_NODE, a["dst"].dtype)
    dst[:edges] = a["dst"]
    m1 = turned(a["Wm1"])
    u = turned(a["Wu"])
    per_layer = [a[k][l] for l in range(LAYERS) for k in ("bu", "gamma", "beta")]
    arrays = {
        "xT": xT,
        "src_tiles": _np.ascontiguousarray(src.reshape(groups * TPG, TILE).T),
        "dst_tiles": _np.ascontiguousarray(dst[:groups * GROUP].reshape(groups * TPG, TILE).T),
        "dst_groups": dst.reshape(128, per_row * GROUP),
        "w_enc": turned(a["W_enc"]),
        "w_out": turned(a["W_out"]),
        "w_m1": by_input(_np.concatenate([m1[:, :FEAT], m1[:, FEAT:]], axis=2)),
        "w_m2": by_input(turned(a["Wm2"])),
        "w_uh": by_input(u[:, :FEAT]),
        "w_ua": by_input(u[:, FEAT:]),
        "cols": _np.ascontiguousarray(_np.stack([a["b_enc"], a["b_out"], *per_layer], axis=1)),
        "bm1": a["bm1"],
        "bm2_row": a["bm2"].reshape(1, LAYERS, FEAT),
    }
    nc = _bacc.Bacc("TRN2", target_bir_lowering=False, num_devices=1)
    d = {k: nc.dram_tensor("in_" + k, v.shape, _mybir.dt.from_np(v.dtype), kind="ExternalInput").ap() for k, v in arrays.items()}
    d["yT"] = nc.dram_tensor("yT", (FEAT, npad), _mybir.dt.float32, kind="ExternalOutput").ap()
    build(nc, d, nodes, edges)
    r = _run(nc, [{"in_" + k: v for k, v in arrays.items()}], core_ids=[0])
    return _np.ascontiguousarray(r.results[0]["yT"][:, :nodes].T)
```

```python
import numpy as np

FEAT = 128
TILE = 128
TPG = 4
GROUP = TILE * TPG
WIN = 128
CHUNK = 256
SUB = CHUNK // 128
SLOTS = 8
HALF = SLOTS // 2
BLOCK = 2 * SLOTS
LEAD = 2
LAYERS = 2
EPS = 1e-5
NO_NODE = 1 << 20


def sizes(nodes, edges):
    groups = -(-edges // GROUP)
    chunks = -(-nodes // CHUNK)
    blocks = (groups - 1) // BLOCK
    beside = max(0, min(blocks - LEAD, chunks))
    return groups, chunks, chunks * CHUNK, -(-groups // 128), -(-nodes // WIN), blocks, beside


def build(nc, d, nodes, edges):
    import concourse.bass as bass
    from concourse import mybir
    from contextlib import ExitStack

    fp32, bf16, i32 = mybir.dt.float32, mybir.dt.bfloat16, mybir.dt.int32
    ALU, ACT = mybir.AluOpType, mybir.ActivationFunctionType
    AX = mybir.AxisListType
    GROUPS, CHUNKS, NPAD, PER_ROW, WINDOWS, BLOCKS, BESIDE = sizes(nodes, edges)
    PARTS = 3
    TOP = NPAD - WIN

    ctx = ExitStack()
    with ctx:
        def sb(name, shape, dt=fp32):
            return ctx.enter_context(nc.sbuf_tensor(name, shape, dt))

        def sem(name):
            return ctx.enter_context(nc.semaphore(name))

        a_table = [nc.dram_tensor(f"a_table{l}", (NPAD, FEAT), fp32, kind="Internal").ap() for l in range(LAYERS)]
        b_table = [nc.dram_tensor(f"b_table{l}", (NPAD, PARTS * FEAT), bf16, kind="Internal").ap() for l in range(LAYERS)]
        base_dram = nc.dram_tensor("base_dram", (128, PER_ROW), fp32, kind="Internal").ap()

        xT = sb("xT", [FEAT, NPAD])
        hT = sb("hT", [FEAT, NPAD])
        acc = sb("acc", [FEAT, NPAD])
        degree = sb("degree", [1, NPAD])
        dst_i = sb("dst_i", [TILE, GROUPS * TPG], i32)
        dst_f = sb("dst_f", [TILE, GROUPS * TPG])
        rel = sb("rel", [TILE, GROUPS * TPG])
        base_all = sb("base_all", [128, 128 * PER_ROW])
        base_row = sb("base_row", [1, 128 * PER_ROW], i32)
        w_enc = sb("w_enc", [FEAT, FEAT])
        w_out = sb("w_out", [FEAT, FEAT])
        w_m1 = sb("w_m1", [FEAT, LAYERS, 2 * FEAT])
        w_m2 = sb("w_m2", [FEAT, LAYERS, FEAT])
        w_uh = sb("w_uh", [FEAT, LAYERS, FEAT])
        w_ua = sb("w_ua", [FEAT, LAYERS, FEAT])
        cols = sb("cols", [FEAT, 2 + 3 * LAYERS])
        bm2_row = sb("bm2_row", [1, LAYERS, FEAT])
        bm1_all = sb("bm1_all", [128, LAYERS, FEAT])
        iota_i = sb("iota_i", [128, 128], i32)
        part_i = sb("part_i", [128, 1], i32)
        win_i = sb("win_i", [128, WINDOWS], i32)
        iota = sb("iota", [128, 128])
        part = sb("part", [128, 1])
        win_start = sb("win_start", [128, WINDOWS])
        ident = sb("ident", [128, 128])
        ones_col = sb("ones_col", [128, 1])
        averager = sb("averager", [128, 128])
        eps_col = sb("eps_col", [128, 1])
        zeros = sb("zeros", [FEAT, CHUNK])
        gmin = sb("gmin", [128, PER_ROW])
        gmax = sb("gmax", [128, PER_ROW])
        base = sb("base", [128, PER_ROW])
        spans = sb("spans", [128, PER_ROW])
        floor = sb("floor", [128, PER_ROW])
        unfit = sb("unfit", [128, 2, PER_ROW])
        unfit_any = sb("unfit_any", [128, 1])
        flag = sb("flag", [1, 1], i32)
        src_ix = sb("src_ix", [TILE, SLOTS, TPG], i32)
        rows = sb("rows", [TILE, SLOTS, GROUP])
        window = sb("window", [WIN, SLOTS, PARTS * FEAT], bf16)
        onehot = sb("onehot", [TILE, 2, GROUP])
        spread = sb("spread", [WIN, 2, GROUP], bf16)
        pre = sb("pre", [TILE, 2, GROUP])
        msg = sb("msg", [TILE, 2, GROUP])
        rel_win = sb("rel_win", [TILE, TPG])
        h_new = sb("h_new", [FEAT, 2, CHUNK])
        a_stage = sb("a_stage", [128, 2, CHUNK])
        b_stage = sb("b_stage", [128, 2, SUB, PARTS, FEAT], bf16)
        b_full = sb("b_full", [128, CHUNK])
        b_rest = sb("b_rest", [128, CHUNK])
        agg_s = sb("agg_s", [FEAT, CHUNK])
        u_s = sb("u_s", [FEAT, CHUNK])
        dev = sb("dev", [FEAT, CHUNK])
        sq = sb("sq", [FEAT, CHUNK])
        std = sb("std", [FEAT, CHUNK])
        rstd = sb("rstd", [FEAT, CHUNK])
        y_out = sb("y_out", [FEAT, CHUNK])
        RUN = PER_ROW * GROUP
        assert 2 * RUN <= SLOTS * GROUP
        flat_rows = rows[:, :, :].rearrange("p s e -> p (s e)")
        dst_g = flat_rows[:, 0:RUN].bitcast(i32)
        dst_gf = flat_rows[:, RUN:2 * RUN]
        dst_gv = flat_rows[:, 0:RUN]

        ps = ctx.enter_context(nc.psum_tensor("ps", [128, 8, 512], fp32))
        flipped, picked, summed_ps = ps[:, 0:2, :], ps[:, 2:4, :], ps[:, 4:6, :]
        by_sub = lambda bank: ps[:, bank, 0:CHUNK].rearrange("p (k f) -> p k f", k=SUB)
        enc_ps = [ps[:, q, 0:CHUNK] for q in range(2)]
        a0_ps, b0_ps = [by_sub(2), by_sub(3)], [by_sub(4), by_sub(5)]
        agg_ps, upd_ps, mean_ps, var_ps = (ps[:, 6 + k % 2, 0:CHUNK] for k in range(4))
        a1_ps, b1_ps = by_sub(6), by_sub(7)

        inputs_in = sem("inputs_in")
        x_in = sem("x_in")
        dst_in = sem("dst_in")
        iotas_made = sem("iotas_made")
        consts_made = sem("consts_made")
        cleared = sem("cleared")
        dve_step = sem("dve_step")
        unfit_found = sem("unfit_found")
        unfit_counted = sem("unfit_counted")
        flag_ready = sem("flag_ready")
        base_found = sem("base_found")
        base_stored = sem("base_stored")
        base_spread = sem("base_spread")
        rows_of_base = sem("rows_of_base")
        rel_ready = sem("rel_ready")
        enc_ready = sem("enc_ready")
        agg_ready = sem("agg_ready")
        agg_copied = sem("agg_copied")
        upd_ready = sem("upd_ready")
        u_ready = sem("u_ready")
        mean_ready = sem("mean_ready")
        dev_ready = sem("dev_ready")
        sq_ready = sem("sq_ready")
        var_ready = sem("var_ready")
        std_ready = sem("std_ready")
        rstd_ready = sem("rstd_ready")
        norm_ready = sem("norm_ready")
        h_ready = sem("h_ready")
        h_kept = sem("h_kept")
        table_ready = sem("table_ready")
        a_staged = sem("a_staged")
        b_full_ready = sem("b_full_ready")
        b_hi_ready = sem("b_hi_ready")
        b_rest_ready = sem("b_rest_ready")
        b_mid_ready = sem("b_mid_ready")
        b_staged = sem("b_staged")
        a0_stored = [sem(f"a0_stored{q}") for q in range(2)]
        b0_stored = [sem(f"b0_stored{q}") for q in range(2)]
        tables_stored = sem("tables_stored")
        a1_stored = sem("a1_stored")
        b1_stored = sem("b1_stored")
        acc_cleared = sem("acc_cleared")
        proj_ready = sem("proj_ready")
        out_ready = sem("out_ready")
        y_stored = sem("y_stored")
        src_ready = [sem(f"src_ready{k}") for k in range(2)]
        rows_ready = [sem(f"rows_ready{k}") for k in range(SLOTS)]
        window_ready = [sem(f"window_ready{k}") for k in range(SLOTS)]
        onehot_ready = sem("onehot_ready")
        flipped_ready = sem("flipped_ready")
        spread_ready = sem("spread_ready")
        picked_ready = sem("picked_ready")
        pre_ready = sem("pre_ready")
        msg_ready = sem("msg_ready")
        summed_ready = sem("summed_ready")
        added = sem("added")
        edges_done = sem("edges_done")
        g_src_ready = sem("g_src_ready")
        g_rows_ready = sem("g_rows_ready")
        g_window_ready = sem("g_window_ready")
        g_rel_ready = sem("g_rel_ready")
        g_onehot_ready = sem("g_onehot_ready")
        g_flipped_ready = sem("g_flipped_ready")
        g_spread_ready = sem("g_spread_ready")
        g_picked_ready = sem("g_picked_ready")
        g_pre_ready = sem("g_pre_ready")
        g_msg_ready = sem("g_msg_ready")
        g_summed_ready = sem("g_summed_ready")
        g_added = sem("g_added")

        WEIGHTS = ("w_enc", "w_m1", "cols", "w_out", "w_m2", "w_uh", "w_ua", "bm2_row", "floor")
        LOADS = 16 * (len(WEIGHTS) + 1)

        block = ctx.enter_context(nc.Block())

        def in_chunks(eng, body):
            pairs = (CHUNKS - 1) // 2
            if pairs:
                with eng.Fori(0, pairs) as i:
                    for q in range(2):
                        body(i * 2 + q, q)
            for c in range(2 * pairs, CHUNKS):
                body(c, c % 2)

        def is_last_chunk(c):
            return isinstance(c, int) and c == CHUNKS - 1

        def in_blocks(eng, body):
            plain = min(LEAD, BLOCKS)
            if plain:
                with eng.Fori(0, plain) as b:
                    body(b, BLOCK, None)
            if BESIDE:
                with eng.Fori(LEAD, LEAD + BESIDE) as b:
                    body(b, BLOCK, b - LEAD)
            for b in range(plain + BESIDE, BLOCKS):
                body(b, BLOCK, None)
            body(BLOCKS, GROUPS - BLOCKS * BLOCK, None)

        def in_rest(eng, first, body):
            if CHUNKS - first > 1:
                with eng.Fori(first, CHUNKS) as c:
                    body(c)
            elif CHUNKS - first == 1:
                body(first)

        def is_last(b, i):
            return isinstance(b, int) and b * BLOCK + i == GROUPS - 1

        def fills(layer, b, i):
            return b * (BLOCK // SLOTS) + i // SLOTS + 1 + layer * -(-(GROUPS - i % SLOTS) // SLOTS)

        def half_fills(layer, b, i):
            first = i % SLOTS // HALF * HALF
            return b * (BLOCK // SLOTS) + i // SLOTS + 1 + layer * -(-(GROUPS - first) // SLOTS)

        def load_starts(engine, b, i, n):
            _, starts = nc.values_load_multi_w_load_instructions(
                base_row[0:1, bass.ds(b * BLOCK + i, min(SLOTS, n - i))], engines=[engine], min_val=0, max_val=TOP,
                skip_runtime_bounds_check_because="the starts were clamped to 0..TOP where they were found")
            return starts

        def chunk(buf, c):
            return buf[:, bass.ds(c * CHUNK, CHUNK)]

        def norms(layer, c, again):
            return c if layer == 0 else CHUNKS + c * 2 + again

        def all_steps(step, layer):
            def body(c):
                for k in range(BLOCK):
                    step(layer, c, k)
            return body

        @block.sync
        def _(sp):
            sp.dma_start(dst_g, d["dst_groups"]).then_inc(dst_in, 16)
            sp.dma_start(xT[:, :], d["xT"]).then_inc(x_in, 16)
            for name, buf in zip(WEIGHTS, (w_enc, w_m1, cols, w_out, w_m2, w_uh, w_ua, bm2_row, floor)):
                view = buf[:, :, :] if len(buf.shape) == 3 else buf[:, :]
                sp.dma_start(view, d[name]).then_inc(inputs_in, 16)
            sp.dma_start(bm1_all[:, :, :], d["bm1"].rearrange("(o l) f -> o l f", o=1).broadcast_to([128, LAYERS, FEAT])
                         ).then_inc(inputs_in, 16)
            sp.dma_start(dst_i[:, :], d["dst_tiles"]).then_inc(dst_in, 16)
            sp.wait_ge(base_found, 1)
            sp.dma_start(base_dram, base[:, :]).then_inc(base_stored, 16)
            sp.wait_ge(base_stored, 16)
            sp.dma_start(base_all[:, :], base_dram.rearrange("(o p) k -> o (p k)", o=1).broadcast_to([128, 128 * PER_ROW])
                         ).then_inc(base_spread, 16)

            def store_tables(c, q):
                to = bass.ds(c * CHUNK, CHUNK)
                sp.wait_ge(a_staged, c + 1)
                sp.nop(nofuse=True)
                sp.dma_start(a_table[0][to, :].rearrange("(k p) f -> p k f", p=128),
                             a_stage[:, q, :].rearrange("p (k f) -> p k f", k=SUB)).then_inc(a0_stored[q], 16)
                sp.wait_ge(b_staged, c + 1 + 2)
                sp.dma_start(b_table[0][to, :].rearrange("(k p) f -> p k f", p=128),
                             b_stage[:, q, :, :, :].rearrange("p k t f -> p k (t f)")).then_inc(b0_stored[q], 16)
                used = (c - q) // 2 + 1
                sp.wait_ge(a0_stored[q], used * 16)
                sp.wait_ge(b0_stored[q], used * 16)
                sp.sem_inc(tables_stored, 1)
            in_chunks(sp, store_tables)

            def few_windows(layer):
                def body(b, n, c):
                    for i in range(n):
                        g, slot = b * BLOCK + i + layer * GROUPS, i % SLOTS
                        if slot == 0:
                            starts = load_starts(mybir.EngineType.SP, b, i, n)
                        if slot % HALF == 0:
                            m = min(HALF, n - i)
                            sp.wait_ge(pre_ready, g + m)
                            sp.nop(nofuse=True)
                            sp.dma_start(src_ix[:, slot:slot + m, :].rearrange("p s t -> p (s t)"),
                                         d["src_tiles"][:, bass.ds((b * BLOCK + i) * TPG, m * TPG)]
                                         ).then_inc(src_ready[slot // HALF], 16)
                        sp.wait_ge(picked_ready, g + 1)
                        sp.dma_start(window[:, slot, :], b_table[layer][bass.ds(starts[slot], WIN), :]
                                     ).then_inc(window_ready[slot], 16)
                in_blocks(sp, body)

            def all_windows(layer):
                with sp.Fori(0, GROUPS) as g:
                    n = g + layer * GROUPS
                    sp.wait_ge(g_added, n * WINDOWS + 1)
                    sp.nop(nofuse=True)
                    sp.dma_start(src_ix[:, 0, :], d["src_tiles"][:, bass.ds(g * TPG, TPG)]).then_inc(g_src_ready, 16)
                    with sp.Fori(0, WINDOWS) as w:
                        sp.wait_ge(g_added, n * WINDOWS + w + 1)
                        sp.nop(nofuse=True)
                        sp.dma_start(window[:, 0, :], b_table[layer][bass.ds(w * WIN, WIN), :]).then_inc(g_window_ready, 16)

            sp.wait_ge(flag_ready, 1)
            many = sp.value_load(flag[0:1, 0:1], min_val=0, max_val=1)
            sp.wait_ge(rows_of_base, 1)
            for layer in range(LAYERS):
                if layer:
                    sp.wait_ge(b1_stored, CHUNKS * 16)
                with sp.If(many == 0):
                    few_windows(layer)
                with sp.Else():
                    all_windows(layer)
            sp.wait_ge(y_stored, CHUNKS * 16)

        @block.gpsimd
        def _(pool):
            pool.iota(iota_i[:, :], pattern=[[1, 128]], base=0, channel_multiplier=0).then_inc(iotas_made, 1)
            pool.iota(part_i[:, :], pattern=[[0, 1]], base=0, channel_multiplier=1).then_inc(iotas_made, 1)
            pool.iota(win_i[:, :], pattern=[[WIN, WINDOWS]], base=0, channel_multiplier=0).then_inc(iotas_made, 1)
            pool.memset(acc[:, :], 0.0).then_inc(cleared, 1)
            pool.memset(degree[:, :], 0.0).then_inc(cleared, 1)

            def keep(c, q):
                pool.wait_ge(h_ready, c + 1)
                pool.tensor_copy(chunk(hT, c), h_new[:, q, :]).then_inc(h_kept, 1)
            in_chunks(pool, keep)

            pool.wait_ge(flag_ready, 1)
            many = pool.value_load(flag[0:1, 0:1], min_val=0, max_val=1)

            def gather(layer, slot, t, done):
                pool.indirect_dma_start(
                    out=rows[:, slot, t * FEAT:(t + 1) * FEAT], out_offset=None, in_=a_table[layer][:, :],
                    in_offset=bass.IndirectOffsetOnAxis(ap=src_ix[:, slot, t:t + 1], axis=0)).then_inc(done, 16)

            def few_windows(layer):
                def body(b, n, c):
                    for i in range(n):
                        slot = i % SLOTS
                        if slot % HALF == 0:
                            pool.wait_ge(src_ready[slot // HALF], half_fills(layer, b, i) * 16)
                            pool.nop(nofuse=True)
                        pool.wait_ge(pre_ready, b * BLOCK + i + layer * GROUPS + 1)
                        pool.nop(nofuse=True)
                        for t in range(TPG):
                            gather(layer, slot, t, rows_ready[slot])
                in_blocks(pool, body)

            def all_windows(layer):
                with pool.Fori(0, GROUPS) as g:
                    pool.wait_ge(g_src_ready, (g + layer * GROUPS + 1) * 16)
                    pool.nop(nofuse=True)
                    for t in range(TPG):
                        gather(layer, 0, t, g_rows_ready)

            for layer in range(LAYERS):
                if layer:
                    pool.wait_ge(a1_stored, CHUNKS * 16)
                else:
                    pool.wait_ge(tables_stored, CHUNKS + 2)
                    pool.nop(nofuse=True)
                    pool.wait_ge(unfit_found, 1)
                pool.nop(nofuse=True)
                with pool.If(many == 0):
                    few_windows(layer)
                with pool.Else():
                    all_windows(layer)

        @block.tensor
        def _(pe):
            def tables(layer, h, a_out, b_out):
                for out, of in ((a_out, 0), (b_out, FEAT)):
                    for k in range(SUB):
                        last = nc.tensor.matmul(out[:, k, :], h[:, k * 128:(k + 1) * 128],
                                                w_m1[:, layer, of:of + FEAT], start=True, stop=True)
                last.then_inc(table_ready, 1)

            def encode(c, q):
                nc.tensor.matmul(enc_ps[q], w_enc[:, :], chunk(xT, c), start=True, stop=True).then_inc(enc_ready, 1)

            def stage0(c, q):
                if not is_last_chunk(c):
                    encode(c + 1, 1 - q)
                pe.wait_ge(h_ready, c + 1)
                pe.wait_ge(b_staged, c + 1)
                tables(0, h_new[:, q, :], a0_ps[q], b0_ps[q])

            pe.wait_ge(inputs_in, LOADS)
            pe.wait_ge(x_in, 16)
            encode(0, 0)
            in_chunks(pe, stage0)
            pe.wait_ge(consts_made, 1)
            pe.wait_ge(unfit_found, 1)
            nc.tensor.matmul(ps[0:1, 7, 0:1], unfit_any[:, :], ones_col[:, :], start=True, stop=True).then_inc(unfit_counted, 1)
            pe.wait_ge(flag_ready, 1)
            many = pe.value_load(flag[0:1, 0:1], min_val=0, max_val=1)
            pe.wait_ge(b_staged, CHUNKS + 2)

            def mean(m):
                pe.wait_ge(u_ready, m + 1)
                nc.tensor.matmul(mean_ps, averager[:, :], u_s[:, :], start=True, stop=True).then_inc(mean_ready, 1)

            def var(m):
                pe.wait_ge(sq_ready, m + 1)
                nc.tensor.matmul(var_ps, averager[:, :], sq[:, :], start=True, stop=True).then_inc(var_ready, 1)

            def step(layer, c, k):
                n = c + layer * CHUNKS
                if k == 0:
                    if layer == 0:
                        pe.wait_ge(b_staged, n + CHUNKS + 2)
                    else:
                        pe.wait_ge(std_ready, norms(layer, c, 0))
                    nc.tensor.matmul(agg_ps, w_m2[:, layer, :], chunk(acc, c), start=True, stop=False)
                    nc.tensor.matmul(agg_ps, bm2_row[:, layer, :], chunk(degree, c), start=False, stop=True
                                     ).then_inc(agg_ready, 1)
                    nc.tensor.matmul(upd_ps, w_uh[:, layer, :], chunk(hT, c), start=True, stop=False)
                elif k == 1:
                    pe.wait_ge(agg_copied, n + 1)
                    nc.tensor.matmul(upd_ps, w_ua[:, layer, :], agg_s[:, :], start=False, stop=True).then_inc(upd_ready, 1)
                elif k == 2:
                    mean(norms(layer, c, 0))
                elif k == 3:
                    var(norms(layer, c, 0))
                elif k == 5:
                    pe.wait_ge(h_ready, n + CHUNKS + 1)
                    if layer == 0:
                        tables(1, h_new[:, 0, :], a1_ps, b1_ps)
                    else:
                        nc.tensor.matmul(agg_ps, w_out[:, :], h_new[:, 0, :], start=True, stop=True).then_inc(proj_ready, 1)
                elif k == 6 and layer == 1:
                    mean(norms(layer, c, 1))
                elif k == 7 and layer == 1:
                    var(norms(layer, c, 1))

            def flip(q, done):
                for t in range(TPG):
                    at = slice(t * 128, (t + 1) * 128)
                    last = nc.tensor.transpose(flipped[:, q, at], onehot[:, q, at], ident[:, :])
                last.then_inc(done, 1)

            def pick(slot, q, done):
                for t in range(TPG):
                    at = slice(t * 128, (t + 1) * 128)
                    for p in range(PARTS):
                        last = nc.tensor.matmul(picked[:, q, at], spread[:, q, at],
                                                window[:, slot, p * FEAT:(p + 1) * FEAT],
                                                start=(p == 0), stop=(p == PARTS - 1))
                last.then_inc(done, 1)

            def count_edges(layer, q):
                for t in range(TPG if layer == 0 else 0):
                    at = slice(t * 128, (t + 1) * 128)
                    nc.tensor.matmul(summed_ps[0:1, q, WIN:2 * WIN], ones_col[:, :], onehot[:, q, at],
                                     start=(t == 0), stop=(t == TPG - 1))

            def sum_up(q, done):
                for t in range(TPG):
                    at = slice(t * 128, (t + 1) * 128)
                    last = nc.tensor.matmul(summed_ps[:, q, 0:WIN], msg[:, q, at], onehot[:, q, at],
                                            start=(t == 0), stop=(t == TPG - 1))
                last.then_inc(done, 1)

            def few_windows(layer):
                def flip_group(g, q):
                    pe.wait_ge(onehot_ready, g + SLOTS + 1)
                    pe.wait_ge(spread_ready, g + SLOTS - 1)
                    flip(q, flipped_ready)

                def body(b, n, c):
                    for i in range(n):
                        g, q = b * BLOCK + i + layer * GROUPS, i % 2
                        pe.wait_ge(spread_ready, g + SLOTS + 1)
                        pe.wait_ge(window_ready[i % SLOTS], fills(layer, b, i) * 16)
                        pe.wait_ge(pre_ready, g + SLOTS - 1)
                        pick(i % SLOTS, q, picked_ready)
                        if not is_last(b, i):
                            flip_group(g + 1, 1 - q)
                        if c is not None:
                            if i == 0:
                                pe.wait_ge(added, g + SLOTS)
                            step(layer, c, i)
                        pe.wait_ge(added, g + SLOTS - 1)
                        count_edges(layer, q)
                        pe.wait_ge(msg_ready, g + SLOTS + 1)
                        sum_up(q, summed_ready)
                flip_group(layer * GROUPS, 0)
                in_blocks(pe, body)
                pe.wait_ge(edges_done, layer + 1)
                in_rest(pe, BESIDE, all_steps(step, layer))

            def all_windows(layer):
                with pe.Fori(0, GROUPS) as g:
                    with pe.Fori(0, WINDOWS) as w:
                        n = (g + layer * GROUPS) * WINDOWS + w
                        pe.wait_ge(g_onehot_ready, n + 1)
                        flip(0, g_flipped_ready)
                        pe.wait_ge(g_spread_ready, n + 1)
                        pe.wait_ge(g_window_ready, n * 16 + 16)
                        pick(0, 0, g_picked_ready)
                        pe.wait_ge(g_msg_ready, n + 1)
                        count_edges(layer, 0)
                        sum_up(0, g_summed_ready)
                pe.wait_ge(edges_done, layer + 1)
                in_rest(pe, 0, all_steps(step, layer))

            for layer in range(LAYERS):
                with pe.If(many == 0):
                    few_windows(layer)
                with pe.Else():
                    all_windows(layer)

        @block.scalar
        def _(act):
            def copy_a(n, q, a_out):
                act.wait_ge(table_ready, n + 1)
                nc.scalar.activation(a_stage[:, q, :].rearrange("p (k f) -> p k f", k=SUB),
                                     a_out, ACT.Copy).then_inc(a_staged, 1)

            def b_hi(n, q):
                act.wait_ge(b_full_ready, n + 1)
                nc.scalar.activation(b_stage[:, q, :, 0, :], b_full[:, :].rearrange("p (k f) -> p k f", k=SUB),
                                     ACT.Copy).then_inc(b_hi_ready, 1)

            def b_mid(n, q):
                act.wait_ge(b_rest_ready, n + 1)
                nc.scalar.activation(b_stage[:, q, :, 1, :], b_rest[:, :].rearrange("p (k f) -> p k f", k=SUB),
                                     ACT.Copy).then_inc(b_mid_ready, 1)

            def encoded(c, q):
                act.wait_ge(enc_ready, c + 1)
                act.wait_ge(h_kept, c + 1)
                nc.scalar.activation(h_new[:, q, :], enc_ps[q], ACT.Identity, bias=cols[:, 0:1]).then_inc(h_ready, 1)

            def stage0(c, q):
                if not is_last_chunk(c):
                    encoded(c + 1, 1 - q)
                act.wait_ge(tables_stored, c + 1)
                copy_a(c, q, a0_ps[q])
                b_hi(c, q)
                b_mid(c, q)

            act.wait_ge(inputs_in, LOADS)
            encoded(0, 0)
            in_chunks(act, stage0)
            act.wait_ge(flag_ready, 1)
            many = act.value_load(flag[0:1, 0:1], min_val=0, max_val=1)

            def square(m):
                act.wait_ge(dev_ready, m + 1)
                nc.scalar.activation(sq[:, :], dev[:, :], ACT.Square).then_inc(sq_ready, 1)

            def root(m):
                act.wait_ge(var_ready, m + 1)
                nc.scalar.activation(std[:, :], var_ps, ACT.Sqrt, bias=eps_col[:, :]).then_inc(std_ready, 1)

            def step(layer, c, k):
                n = c + layer * CHUNKS
                to = bass.ds(c * CHUNK, CHUNK)
                if k == 0:
                    act.wait_ge(agg_ready, n + 1)
                    nc.scalar.activation(agg_s[:, :], agg_ps, ACT.Copy).then_inc(agg_copied, 1)
                elif k == 2:
                    square(norms(layer, c, 0))
                elif k == 3:
                    root(norms(layer, c, 0))
                elif k == 5 and layer == 0:
                    act.wait_ge(h_ready, n + CHUNKS + 1)
                    nc.scalar.activation(chunk(hT, c), h_new[:, 0, :], ACT.Copy).then_inc(h_kept, 1)
                    copy_a(n + CHUNKS, 0, a1_ps)
                elif k == 6 and layer == 0:
                    act.wait_ge(a_staged, n + CHUNKS + 1)
                    act.dma_start(a_table[1][to, :].rearrange("(k p) f -> p k f", p=128),
                                  a_stage[:, 0, :].rearrange("p (k f) -> p k f", k=SUB)).then_inc(a1_stored, 16)
                    b_hi(n + CHUNKS, 0)
                elif k == 7 and layer == 0:
                    b_mid(n + CHUNKS, 0)
                elif k == 9 and layer == 0:
                    act.wait_ge(b_staged, n + CHUNKS + 1 + 2)
                    act.dma_start(b_table[1][to, :].rearrange("(k p) f -> p k f", p=128),
                                  b_stage[:, 0, :, :, :].rearrange("p k t f -> p k (t f)")).then_inc(b1_stored, 16)
                elif k == 12 and layer == 0:
                    act.wait_ge(a1_stored, (c + 1) * 16)
                    act.wait_ge(b1_stored, (c + 1) * 16)
                elif k == 6:
                    square(norms(layer, c, 1))
                elif k == 7:
                    root(norms(layer, c, 1))
                elif k == 9:
                    act.wait_ge(out_ready, c + 1)
                    act.dma_start(d["yT"][:, to], y_out[:, :]).then_inc(y_stored, 16)
                elif k == 12:
                    act.wait_ge(y_stored, (c + 1) * 16)

            def few_windows(layer):
                def spread_group(g, q):
                    act.wait_ge(flipped_ready, g + SLOTS + 1)
                    act.wait_ge(picked_ready, g + SLOTS - 1)
                    nc.scalar.activation(spread[:, q, :], flipped[:, q, :], ACT.Copy).then_inc(spread_ready, 1)

                def body(b, n, c):
                    for i in range(n):
                        g, q = b * BLOCK + i + layer * GROUPS, i % 2
                        act.wait_ge(pre_ready, g + SLOTS + 1)
                        act.wait_ge(summed_ready, g + SLOTS - 1)
                        nc.scalar.activation(msg[:, q, :], pre[:, q, :], ACT.Relu).then_inc(msg_ready, 1)
                        if not is_last(b, i):
                            spread_group(g + 1, 1 - q)
                        if c is not None:
                            step(layer, c, i)
                spread_group(layer * GROUPS, 0)
                in_blocks(act, body)
                in_rest(act, BESIDE, all_steps(step, layer))

            def all_windows(layer):
                with act.Fori(0, GROUPS) as g:
                    with act.Fori(0, WINDOWS) as w:
                        n = (g + layer * GROUPS) * WINDOWS + w
                        act.wait_ge(g_flipped_ready, n + 1)
                        nc.scalar.activation(spread[:, 0, :], flipped[:, 0, :], ACT.Copy).then_inc(g_spread_ready, 1)
                        act.wait_ge(g_pre_ready, n + 1)
                        nc.scalar.activation(msg[:, 0, :], pre[:, 0, :], ACT.Relu).then_inc(g_msg_ready, 1)
                in_rest(act, 0, all_steps(step, layer))

            for layer in range(LAYERS):
                with act.If(many == 0):
                    few_windows(layer)
                with act.Else():
                    all_windows(layer)

        @block.vector
        def _(dve):
            steps = [0]

            def link(ins):
                steps[0] += 1
                ins.then_inc(dve_step, 1)
                dve.wait_ge(dve_step, steps[0])

            for ring in (onehot_ready, flipped_ready, spread_ready, picked_ready, pre_ready, msg_ready,
                         summed_ready, added):
                dve.sem_inc(ring, SLOTS)
            for ring in (b_staged, tables_stored, h_kept):
                dve.sem_inc(ring, 2)
            dve.sem_inc(g_added, 1)

            nc.vector.memset(ones_col[:, :], 1.0)
            nc.vector.memset(averager[:, :], 1.0 / FEAT)
            nc.vector.memset(eps_col[:, :], EPS)
            nc.vector.memset(zeros[:, :], 0.0)
            dve.wait_ge(iotas_made, 3)
            nc.vector.tensor_copy(iota[:, :], iota_i[:, :])
            nc.vector.tensor_copy(win_start[:, :], win_i[:, :])
            link(nc.vector.tensor_copy(part[:, :], part_i[:, :]))
            nc.vector.tensor_scalar(ident[:, :], iota[:, :], part[:, 0:1], None, ALU.is_equal).then_inc(consts_made, 1)

            dve.wait_ge(dst_in, 16 * 2)
            link(nc.vector.tensor_copy(dst_gf, dst_g))
            by_group = lambda buf: buf.rearrange("p (k e) -> p k e", e=GROUP)
            nc.vector.tensor_reduce(gmin[:, :], by_group(dst_gf), AX.X, ALU.min)
            link(nc.vector.scalar_tensor_tensor(dst_gv, dst_gf, float(NO_NODE), dst_gf, ALU.is_lt, ALU.mult))
            nc.vector.tensor_reduce(gmax[:, :], by_group(dst_gv), AX.X, ALU.max)
            nc.vector.tensor_scalar(base[:, :], gmin[:, :], float(TOP), 0.0, ALU.min, ALU.max).then_inc(base_found, 1)
            dve.wait_ge(base_found, 1)
            dve.wait_ge(inputs_in, LOADS)
            nc.vector.tensor_tensor(unfit[:, 1, :], floor[:, :], base[:, :], ALU.is_gt)
            link(nc.vector.tensor_tensor(spans[:, :], gmax[:, :], base[:, :], ALU.subtract))
            link(nc.vector.tensor_scalar(unfit[:, 0, :], spans[:, :], float(WIN), None, ALU.is_ge))
            nc.vector.tensor_reduce(unfit_any[:, :], unfit[:, :, :], AX.XY, ALU.max).then_inc(unfit_found, 1)

            def b_full_step(stage, n, b_out):
                dve.wait_ge(table_ready, n + 1)
                nc.vector.tensor_tensor(b_full[:, :].rearrange("p (k f) -> p k f", k=SUB), b_out,
                                        bm1_all[:, stage:stage + 1, :].broadcast_to([128, SUB, FEAT]),
                                        ALU.add).then_inc(b_full_ready, 1)

            def b_rest_step(n, q):
                dve.wait_ge(b_hi_ready, n + 1)
                nc.vector.tensor_tensor(b_rest[:, :].rearrange("p (k f) -> p k f", k=SUB),
                                        b_full[:, :].rearrange("p (k f) -> p k f", k=SUB), b_stage[:, q, :, 0, :],
                                        ALU.subtract).then_inc(b_rest_ready, 1)

            def b_lo_step(n, q):
                dve.wait_ge(b_mid_ready, n + 1)
                nc.vector.tensor_tensor(b_stage[:, q, :, 2, :], b_rest[:, :].rearrange("p (k f) -> p k f", k=SUB),
                                        b_stage[:, q, :, 1, :], ALU.subtract).then_inc(b_staged, 1)

            def stage0(c, q):
                b_full_step(0, c, b0_ps[q])
                b_rest_step(c, q)
                b_lo_step(c, q)
            in_chunks(dve, stage0)

            dve.wait_ge(unfit_counted, 1)
            nc.vector.tensor_scalar(flag[:, :], ps[0:1, 7, 0:1], 0.0, None, ALU.is_gt).then_inc(flag_ready, 1)
            dve.wait_ge(flag_ready, 1)
            many = dve.value_load(flag[0:1, 0:1], min_val=0, max_val=1)
            dve.wait_ge(base_spread, 16)
            nc.vector.tensor_copy(base_row[:, :], base_all[0:1, :]).then_inc(rows_of_base, 1)
            dve.wait_ge(rows_of_base, 1)
            link(nc.vector.tensor_copy(dst_f[:, :], dst_i[:, :]))
            nc.vector.tensor_tensor(rel[:, :].rearrange("p (g t) -> p g t", t=TPG),
                                    dst_f[:, :].rearrange("p (g t) -> p g t", t=TPG),
                                    base_all[:, 0:GROUPS].rearrange("p (g o) -> p g o", o=1).broadcast_to([128, GROUPS, TPG]),
                                    ALU.subtract).then_inc(rel_ready, 1)
            dve.wait_ge(rel_ready, 1)
            dve.wait_ge(cleared, 2)

            def deviation(m):
                dve.wait_ge(mean_ready, m + 1)
                nc.vector.tensor_tensor(dev[:, :], u_s[:, :], mean_ps, ALU.subtract).then_inc(dev_ready, 1)

            def inverse(m):
                dve.wait_ge(std_ready, m + 1)
                nc.vector.reciprocal(rstd[:, :], std[:, :]).then_inc(rstd_ready, 1)
                dve.wait_ge(rstd_ready, m + 1)

            def step(layer, c, k):
                n = c + layer * CHUNKS
                bu, gamma, beta = (cols[:, 2 + 3 * layer + j:3 + 3 * layer + j] for j in range(3))
                if k == 1:
                    dve.wait_ge(upd_ready, n + 1)
                    nc.vector.scalar_tensor_tensor(u_s[:, :], upd_ps, bu, chunk(hT, c), ALU.add, ALU.add).then_inc(u_ready, 1)
                    if layer + 1 < LAYERS:
                        nc.vector.tensor_copy(chunk(acc, c), zeros[:, :]).then_inc(acc_cleared, 1)
                elif k == 2:
                    deviation(norms(layer, c, 0))
                elif k == 4:
                    inverse(norms(layer, c, 0))
                    nc.vector.tensor_tensor(rstd[:, :], rstd[:, :], dev[:, :], ALU.mult).then_inc(norm_ready, 1)
                    dve.wait_ge(h_kept, (c + 1 if layer == 0 else CHUNKS + 1) + CHUNKS + 1)
                    dve.wait_ge(norm_ready, n + 1)
                    nc.vector.tensor_scalar(h_new[:, 0, :], rstd[:, :], gamma, beta, ALU.mult, ALU.add).then_inc(h_ready, 1)
                elif k == 5 and layer == 0:
                    b_full_step(1, n + CHUNKS, b1_ps)
                elif k == 7 and layer == 0:
                    b_rest_step(n + CHUNKS, 0)
                elif k == 8 and layer == 0:
                    b_lo_step(n + CHUNKS, 0)
                elif k == 5:
                    dve.wait_ge(proj_ready, c + 1)
                    nc.vector.scalar_tensor_tensor(u_s[:, :], agg_ps, cols[:, 1:2], chunk(xT, c), ALU.add, ALU.add
                                                   ).then_inc(u_ready, 1)
                elif k == 6 and layer == 1:
                    deviation(norms(layer, c, 1))
                elif k == 8:
                    inverse(norms(layer, c, 1))
                    nc.vector.tensor_tensor(y_out[:, :], rstd[:, :], dev[:, :], ALU.mult).then_inc(out_ready, 1)

            def one_hots(rel_cols, q):
                return nc.vector.tensor_tensor(
                    onehot[:, q, :].rearrange("p (t n) -> p t n", t=TPG),
                    iota[:, :].rearrange("p (o n) -> p o n", o=1).broadcast_to([TILE, TPG, WIN]),
                    rel_cols.rearrange("p (t o) -> p t o", o=1).broadcast_to([TILE, TPG, WIN]), ALU.is_equal)

            def add_sums(layer, start, q, done):
                at = bass.ds(start, WIN)
                last = nc.vector.tensor_tensor(acc[:, at], acc[:, at], summed_ps[:, q, 0:WIN], ALU.add)
                if layer == 0:
                    last = nc.vector.tensor_tensor(degree[:, at], degree[:, at], summed_ps[0:1, q, WIN:2 * WIN], ALU.add)
                last.then_inc(done, 1)

            def few_windows(layer):
                def onehot_group(g_in_layer, q):
                    dve.wait_ge(summed_ready, g_in_layer + layer * GROUPS + SLOTS - 1)
                    one_hots(rel[:, bass.ds(g_in_layer * TPG, TPG)], q).then_inc(onehot_ready, 1)

                def body(b, n, c):
                    for i in range(n):
                        g, q, slot = b * BLOCK + i + layer * GROUPS, i % 2, i % SLOTS
                        if slot == 0:
                            starts = load_starts(mybir.EngineType.DVE, b, i, n)
                        if not is_last(b, i):
                            onehot_group(b * BLOCK + i + 1, 1 - q)
                        dve.wait_ge(rows_ready[slot], fills(layer, b, i) * (16 * TPG))
                        dve.wait_ge(picked_ready, g + SLOTS + 1)
                        dve.wait_ge(msg_ready, g + SLOTS - 1)
                        nc.vector.tensor_tensor(pre[:, q, :], rows[:, slot, :], picked[:, q, :], ALU.add
                                                ).then_inc(pre_ready, 1)
                        if c is not None:
                            step(layer, c, i)
                        dve.wait_ge(summed_ready, g + SLOTS + 1)
                        dve.wait_ge(added, g + SLOTS)
                        add_sums(layer, starts[slot], q, added)
                onehot_group(0, 0)
                in_blocks(dve, body)
                dve.wait_ge(added, (layer + 1) * GROUPS + SLOTS)
                dve.sem_inc(edges_done, 1)
                in_rest(dve, BESIDE, all_steps(step, layer))

            def all_windows(layer):
                with dve.Fori(0, GROUPS) as g:
                    with dve.Fori(0, WINDOWS) as w:
                        n = (g + layer * GROUPS) * WINDOWS + w
                        nc.vector.tensor_scalar(rel_win[:, :], dst_f[:, bass.ds(g * TPG, TPG)],
                                                win_start[:, bass.ds(w, 1)], None, ALU.subtract).then_inc(g_rel_ready, 1)
                        dve.wait_ge(g_rel_ready, n + 1)
                        one_hots(rel_win[:, :], 0).then_inc(g_onehot_ready, 1)
                        dve.wait_ge(g_rows_ready, (g + layer * GROUPS + 1) * (16 * TPG))
                        dve.wait_ge(g_picked_ready, n + 1)
                        nc.vector.tensor_tensor(pre[:, 0, :], rows[:, 0, :], picked[:, 0, :], ALU.add
                                                ).then_inc(g_pre_ready, 1)
                        dve.wait_ge(g_summed_ready, n + 1)
                        add_sums(layer, w * WIN, 0, g_added)
                        dve.wait_ge(g_added, n + 2)
                dve.sem_inc(edges_done, 1)
                in_rest(dve, 0, all_steps(step, layer))

            for layer in range(LAYERS):
                with dve.If(many == 0):
                    few_windows(layer)
                with dve.Else():
                    all_windows(layer)


def kernel(**inputs):
    import numpy as _np
    import concourse.bacc as _bacc
    from concourse import mybir as _mybir
    from concourse.bass_utils import run_bass_kernel_spmd as _run

    a = {k.removeprefix("L0_gnn_"): _np.asarray(v) for k, v in inputs.items()}
    nodes, edges = a["x"].shape[0], a["src"].shape[0]
    groups, chunks, npad, per_row, _, blocks, beside = sizes(nodes, edges)

    def turned(w):
        return _np.ascontiguousarray(_np.swapaxes(w, -1, -2))

    def by_input(w):
        return _np.ascontiguousarray(_np.swapaxes(w, 0, 1))

    xT = _np.zeros((FEAT, npad), a["x"].dtype)
    xT[:, :nodes] = a["x"].T
    src = _np.zeros(groups * GROUP, a["src"].dtype)
    src[:edges] = a["src"]
    dst = _np.full(128 * per_row * GROUP, NO_NODE, a["dst"].dtype)
    dst[:edges] = a["dst"]
    begun = _np.clip(_np.arange(128 * per_row) // BLOCK - LEAD + 1, 0, beside)
    m1 = turned(a["Wm1"])
    u = turned(a["Wu"])
    per_layer = [a[k][l] for l in range(LAYERS) for k in ("bu", "gamma", "beta")]
    arrays = {
        "xT": xT,
        "src_tiles": _np.ascontiguousarray(src.reshape(groups * TPG, TILE).T),
        "dst_tiles": _np.ascontiguousarray(dst[:groups * GROUP].reshape(groups * TPG, TILE).T),
        "dst_groups": dst.reshape(128, per_row * GROUP),
        "w_enc": turned(a["W_enc"]),
        "w_out": turned(a["W_out"]),
        "w_m1": by_input(_np.concatenate([m1[:, :FEAT], m1[:, FEAT:]], axis=2)),
        "w_m2": by_input(turned(a["Wm2"])),
        "w_uh": by_input(u[:, :FEAT]),
        "w_ua": by_input(u[:, FEAT:]),
        "cols": _np.ascontiguousarray(_np.stack([a["b_enc"], a["b_out"], *per_layer], axis=1)),
        "floor": (begun * CHUNK).astype(_np.float32).reshape(128, per_row),
        "bm1": a["bm1"],
        "bm2_row": a["bm2"].reshape(1, LAYERS, FEAT),
    }
    nc = _bacc.Bacc("TRN2", target_bir_lowering=False, num_devices=1)
    d = {k: nc.dram_tensor("in_" + k, v.shape, _mybir.dt.from_np(v.dtype), kind="ExternalInput").ap() for k, v in arrays.items()}
    d["yT"] = nc.dram_tensor("yT", (FEAT, npad), _mybir.dt.float32, kind="ExternalOutput").ap()
    build(nc, d, nodes, edges)
    r = _run(nc, [{"in_" + k: v for k, v in arrays.items()}], core_ids=[0])
    return _np.ascontiguousarray(r.results[0]["yT"][:, :nodes].T)
```

```python
import numpy as np

FEAT = 128
TILE = 128
TPG = 4
GROUP = TILE * TPG
WIN = 128
CHUNK = 256
WIDE = 512
SLOTS = 16
IX_PART = 4
WIN_SLOTS = 8
BLOCK = SLOTS
LEAD = 2
LAYERS = 2
EPS = 1e-5
NO_NODE = 1 << 20


def sizes(nodes, edges):
    groups = -(-edges // GROUP)
    npad = -(-nodes // WIN) * WIN
    chunks = -(-npad // CHUNK)
    blocks = (groups - 1) // BLOCK
    beside = max(0, min(blocks - LEAD, chunks - 1))
    tail = int(beside == blocks - LEAD and 0 < beside < chunks - 1)
    return groups, npad, -(-groups // 128), chunks, -(-npad // WIDE), blocks, beside, tail


def build(nc, d, nodes, edges):
    import concourse.bass as bass
    from concourse import mybir
    from contextlib import ExitStack

    fp32, bf16, i32 = mybir.dt.float32, mybir.dt.bfloat16, mybir.dt.int32
    ALU, ACT = mybir.AluOpType, mybir.ActivationFunctionType
    AX = mybir.AxisListType
    GROUPS, NPAD, PER_ROW, CHUNKS, WIDES, BLOCKS, BESIDE, TAIL = sizes(nodes, edges)
    WINDOWS = NPAD // WIN
    PARTS = 3
    TAIL_GROUPS = GROUPS - BLOCKS * BLOCK
    TOP = NPAD - WIN

    ctx = ExitStack()
    with ctx:
        def sb(name, shape, dt=fp32):
            return ctx.enter_context(nc.sbuf_tensor(name, shape, dt))

        def sem(name):
            return ctx.enter_context(nc.semaphore(name))

        a_table = [nc.dram_tensor(f"a_table{l}", (NPAD, FEAT), fp32, kind="Internal").ap() for l in range(LAYERS)]
        b_table = [nc.dram_tensor(f"b_table{l}", (NPAD, PARTS * FEAT), bf16, kind="Internal").ap() for l in range(LAYERS)]
        base_dram = nc.dram_tensor("base_dram", (128, PER_ROW), fp32, kind="Internal").ap()

        xT = sb("xT", [FEAT, NPAD])
        hT = sb("hT", [FEAT, NPAD])
        acc = sb("acc", [FEAT, NPAD])
        degree = sb("degree", [1, NPAD])
        dst_i = sb("dst_i", [TILE, GROUPS * TPG], i32)
        dst_f = sb("dst_f", [TILE, GROUPS * TPG])
        rel = dst_i[:, :].bitcast(fp32)
        base_all = sb("base_all", [128, 128 * PER_ROW])
        base_row = sb("base_row", [1, 128 * PER_ROW], i32)
        w_enc = sb("w_enc", [FEAT, FEAT])
        w_enc_out = sb("w_enc_out", [FEAT, FEAT])
        w_a0 = sb("w_a0", [FEAT, FEAT])
        b_enc_all = sb("b_enc_all", [FEAT, 128])
        w_out = sb("w_out", [FEAT, FEAT])
        w_m1 = sb("w_m1", [FEAT, LAYERS, 2 * FEAT])
        w_m2 = sb("w_m2", [FEAT, LAYERS, FEAT])
        w_uh = sb("w_uh", [FEAT, LAYERS, FEAT])
        w_ua = sb("w_ua", [FEAT, LAYERS, FEAT])
        cols = sb("cols", [FEAT, 2 + 3 * LAYERS])
        bm2_row = sb("bm2_row", [1, LAYERS, FEAT])
        bm1_all = sb("bm1_all", [128, LAYERS, FEAT])
        iota_i = sb("iota_i", [128, 128], i32)
        part_i = sb("part_i", [128, 1], i32)
        win_i = sb("win_i", [128, WINDOWS], i32)
        iota = sb("iota", [128, 128])
        part = sb("part", [128, 1])
        win_start = sb("win_start", [128, WINDOWS])
        ident = sb("ident", [128, 128])
        ones_col = sb("ones_col", [128, 1])
        averager = sb("averager", [128, 128])
        eps_col = sb("eps_col", [128, 1])
        zeros = sb("zeros", [FEAT, CHUNK])
        gmin = sb("gmin", [128, PER_ROW])
        gmax = sb("gmax", [128, PER_ROW])
        base = sb("base", [128, PER_ROW])
        spans = sb("spans", [128, PER_ROW])
        floor = sb("floor", [128, PER_ROW])
        unfit = sb("unfit", [128, 2, PER_ROW])
        unfit_any = sb("unfit_any", [128, 1])
        flag = sb("flag", [1, 1], i32)
        src_ix = sb("src_ix", [TILE, SLOTS, TPG], i32)
        rows = sb("rows", [TILE, SLOTS, GROUP])
        window = sb("window", [WIN, WIN_SLOTS, PARTS * FEAT], bf16)
        onehot = sb("onehot", [TILE, 4, GROUP])
        spread = sb("spread", [WIN, 2, GROUP], bf16)
        pre = sb("pre", [TILE, 2, GROUP])
        msg = sb("msg", [TILE, 2, GROUP])
        rel_win = sb("rel_win", [TILE, TPG])
        h_new = sb("h_new", [FEAT, 2, WIDE])
        a_stage = sb("a_stage", [128, CHUNK // 128, FEAT])
        b_stage = sb("b_stage", [128, 2, WIDE // 128, PARTS, FEAT], bf16)
        b_full = sb("b_full", [128, 2, WIDE // 128, FEAT])
        b_rest = sb("b_rest", [128, 2, WIDE // 128, FEAT])
        flat = lambda buf: buf[:, 1, :, :].rearrange("p k f -> p (k f)")
        agg_s, u_s = h_new[:, 1, 0:CHUNK], h_new[:, 1, CHUNK:2 * CHUNK]
        dev, sq = flat(b_full)[:, 0:CHUNK], flat(b_full)[:, CHUNK:2 * CHUNK]
        std, rstd = flat(b_rest)[:, 0:CHUNK], flat(b_rest)[:, CHUNK:2 * CHUNK]
        y_out = sb("y_out", [FEAT, CHUNK])
        a0_stage = hT[:, :].rearrange("p (k f) -> p k f", f=FEAT)
        RUN = PER_ROW * GROUP
        assert 2 * RUN <= SLOTS * GROUP
        flat_rows = rows[:, :, :].rearrange("p s e -> p (s e)")
        dst_g = flat_rows[:, 0:RUN].bitcast(i32)
        dst_gf = flat_rows[:, RUN:2 * RUN]
        dst_gv = flat_rows[:, 0:RUN]

        ps = ctx.enter_context(nc.psum_tensor("ps", [128, 8, 512], fp32))
        flipped, picked, summed_ps = ps[:, 0:2, :], ps[:, 2:4, :], ps[:, 4:6, :]
        by_part = lambda bank: ps[:, bank, :].rearrange("p (k f) -> p k f", f=FEAT)
        enc_ps = [ps[:, q, :] for q in range(2)]
        a0_ps, b0_ps = [by_part(2), by_part(3)], [by_part(4), by_part(5)]
        agg_ps, upd_ps, mean_ps, var_ps = (ps[:, 6 + k % 2, 0:CHUNK] for k in range(4))
        a1_ps, b1_ps = by_part(6), by_part(7)

        early_in = sem("early_in")
        late_in = sem("late_in")
        x_in = [sem(f"x_in{k}") for k in range(-(-WIDES // 3))]
        dst_g_in = sem("dst_g_in")
        dst_in = sem("dst_in")
        iotas_made = sem("iotas_made")
        consts_made = sem("consts_made")
        cleared = sem("cleared")
        dve_step = sem("dve_step")
        unfit_found = sem("unfit_found")
        unfit_counted = sem("unfit_counted")
        flag_ready = sem("flag_ready")
        base_found = sem("base_found")
        base_stored = sem("base_stored")
        base_spread = sem("base_spread")
        rows_of_base = sem("rows_of_base")
        rel_ready = sem("rel_ready")
        w_a0_ready = sem("w_a0_ready")
        w_a0_kept = sem("w_a0_kept")
        b_enc_spread = sem("b_enc_spread")
        b_bias_ready = sem("b_bias_ready")
        b_bias_kept = sem("b_bias_kept")
        a0_ready = sem("a0_ready")
        a0_staged = sem("a0_staged")
        enc_ready = sem("enc_ready")
        agg_ready = sem("agg_ready")
        agg_copied = sem("agg_copied")
        upd_ready = sem("upd_ready")
        u_ready = sem("u_ready")
        mean_ready = sem("mean_ready")
        dev_ready = sem("dev_ready")
        sq_ready = sem("sq_ready")
        var_ready = sem("var_ready")
        std_ready = sem("std_ready")
        rstd_ready = sem("rstd_ready")
        norm_ready = sem("norm_ready")
        h_ready = sem("h_ready")
        h_kept = sem("h_kept")
        table_ready = sem("table_ready")
        a_staged = sem("a_staged")
        b_full_ready = sem("b_full_ready")
        b_hi_ready = sem("b_hi_ready")
        b_rest_ready = sem("b_rest_ready")
        b_mid_ready = sem("b_mid_ready")
        b_staged = sem("b_staged")
        a0_stored = sem("a0_stored")
        b0_stored = [sem(f"b0_stored{q}") for q in range(2)]
        a1_stored = sem("a1_stored")
        b1_stored = sem("b1_stored")
        acc_cleared = sem("acc_cleared")
        proj_ready = sem("proj_ready")
        out_ready = sem("out_ready")
        y_stored = sem("y_stored")
        src_ready = [sem(f"src_ready{k}") for k in range(SLOTS // IX_PART)]
        rows_ready = [sem(f"rows_ready{k}") for k in range(SLOTS)]
        window_ready = [sem(f"window_ready{k}") for k in range(WIN_SLOTS)]
        onehot_ready = sem("onehot_ready")
        flipped_ready = sem("flipped_ready")
        spread_ready = sem("spread_ready")
        picked_ready = sem("picked_ready")
        pre_ready = sem("pre_ready")
        msg_ready = sem("msg_ready")
        summed_ready = sem("summed_ready")
        added = sem("added")
        edges_done = sem("edges_done")
        g_src_ready = sem("g_src_ready")
        g_rows_ready = sem("g_rows_ready")
        g_window_ready = sem("g_window_ready")
        g_rel_ready = sem("g_rel_ready")
        g_onehot_ready = sem("g_onehot_ready")
        g_flipped_ready = sem("g_flipped_ready")
        g_spread_ready = sem("g_spread_ready")
        g_picked_ready = sem("g_picked_ready")
        g_pre_ready = sem("g_pre_ready")
        g_msg_ready = sem("g_msg_ready")
        g_summed_ready = sem("g_summed_ready")
        g_added = sem("g_added")

        X_PART = 3
        WEIGHTS = {"w_enc": w_enc, "w_out": w_out, "w_m1": w_m1, "w_m2": w_m2, "w_uh": w_uh, "w_ua": w_ua,
                   "w_enc_out": w_enc_out, "cols": cols, "bm2_row": bm2_row, "floor": floor}
        EARLY_LOADS, LATE_LOADS = 16 * 5, 16 * 6

        def load(eng, names, done):
            for name in names:
                buf = WEIGHTS[name]
                eng.dma_start(buf[:, :, :] if len(buf.shape) == 3 else buf[:, :], d[name]).then_inc(done, 16)

        block = ctx.enter_context(nc.Block())

        def in_wides(eng, body):
            pairs = max(1, (WIDES - 2) // 2)
            for c in range(min(2, WIDES)):
                body(c, c, 0, width(c))
            if pairs > 1:
                with eng.Fori(1, pairs) as i:
                    for q in range(2):
                        body(i * 2 + q, q, i, WIDE)
            for c in range(2 * pairs, WIDES):
                body(c, c % 2, c // 2, width(c))

        def width(c):
            return NPAD - c * WIDE if isinstance(c, int) and c == WIDES - 1 else WIDE

        def is_last_wide(c):
            return isinstance(c, int) and c == WIDES - 1

        def early(c):
            return isinstance(c, int) and c < 2

        def in_blocks(eng, body):
            plain = min(LEAD, BLOCKS)
            looped = BLOCKS - (TAIL_GROUPS == 1)
            for first, stop, beside in ((0, plain, False), (LEAD, LEAD + BESIDE, True)):
                loop_stop = max(first, min(stop, looped))
                if loop_stop > first:
                    with eng.Fori(first, loop_stop) as b:
                        body(b, BLOCK, b - LEAD if beside else None)
                for b in range(loop_stop, stop):
                    body(b, BLOCK, b - LEAD if beside else None)
            for b in range(plain + BESIDE, BLOCKS):
                body(b, BLOCK, None)
            body(BLOCKS, TAIL_GROUPS, BESIDE if TAIL else None)

        def steps_beside(i, n):
            return range(i * BLOCK // n, (i + 1) * BLOCK // n)

        def in_rest(eng, first, step, layer):
            def body(c, w):
                for k in range(BLOCK):
                    step(layer, c, k, w)
            if CHUNKS - 1 > first:
                with eng.Fori(first, CHUNKS - 1) as c:
                    body(c, CHUNK)
            body(CHUNKS - 1, NPAD - (CHUNKS - 1) * CHUNK)

        def there_is(b, i):
            return not isinstance(b, int) or b * BLOCK + i < GROUPS

        def fills(layer, b, i, slots):
            return b * (BLOCK // slots) + i // slots + 1 + layer * -(-(GROUPS - i % slots) // slots)

        def refills(b, i):
            return i % IX_PART == IX_PART - 1 and not (isinstance(b, int) and b == BLOCKS)

        def part_fills(layer, b):
            return b + 1 + layer * (BLOCKS + 1)

        def load_starts(engine, b, i, n):
            _, starts = nc.values_load_multi_w_load_instructions(
                base_row[0:1, bass.ds(b * BLOCK + i, min(WIN_SLOTS, n - i))], engines=[engine], min_val=0, max_val=TOP,
                skip_runtime_bounds_check_because="the starts were clamped to 0..TOP where they were found")
            return starts

        def chunk(buf, c, w):
            return buf[:, bass.ds(c * CHUNK, w)]

        def wide(buf, c, w):
            return buf[:, bass.ds(c * WIDE, w)]

        def norms(layer, c, again):
            return c if layer == 0 else CHUNKS + c * 2 + again

        def by_node(table, start, w):
            return table[bass.ds(start, w), :].rearrange("(k p) f -> p k f", p=128)

        def a_rows(w):
            return a_stage[:, 0:w // 128, :]

        def b_rows(q, w):
            return b_stage[:, q, 0:w // 128, :, :].rearrange("p k t f -> p k (t f)")

        @block.sync
        def _(sp):
            def load_x(k):
                to = slice(k * X_PART * WIDE, min((k + 1) * X_PART * WIDE, NPAD))
                sp.dma_start(xT[:, to], d["xT"][:, to]).then_inc(x_in[k], 16)

            load_x(0)
            sp.wait_ge(early_in, EARLY_LOADS)
            sp.dma_start(dst_g, d["dst_groups"]).then_inc(dst_g_in, 16)
            for k in range(1, len(x_in)):
                load_x(k)
            sp.dma_start(dst_i[:, :], d["dst_tiles"]).then_inc(dst_in, 16)
            load(sp, ("w_enc", "w_out", "w_m2", "w_uh", "w_ua", "bm2_row"), late_in)
            for c in range(WIDES):
                w = width(c)
                sp.wait_ge(a0_staged, c + 1)
                sp.dma_start(by_node(a_table[0], c * WIDE, w), a0_stage[:, c * WIDE // 128:(c * WIDE + w) // 128, :]
                             ).then_inc(a0_stored, 16)
            sp.wait_ge(base_found, 1)
            sp.dma_start(base_dram, base[:, :]).then_inc(base_stored, 16)

            def spread_base():
                sp.wait_ge(base_stored, 16)
                sp.dma_start(base_all[:, :], base_dram.rearrange("(o p) k -> o (p k)", o=1).broadcast_to([128, 128 * PER_ROW])
                             ).then_inc(base_spread, 16)

            def few_windows(layer):
                def body(b, n, c):
                    for i in range(n):
                        g, slot = b * BLOCK + i + layer * GROUPS, i % WIN_SLOTS
                        if i == 0:
                            sp.wait_ge(rows_of_base, 1)
                        if slot == 0:
                            starts = load_starts(mybir.EngineType.SP, b, i, n)
                        if i == 0:
                            for q in range(2) if layer == 0 else ():
                                sp.wait_ge(b0_stored[q], 16 * ((WIDES + 1 - q) // 2))
                            if layer:
                                sp.wait_ge(b1_stored, CHUNKS * 16)
                        sp.wait_ge(picked_ready, g + SLOTS - WIN_SLOTS + 1)
                        sp.dma_start(window[:, slot, :], b_table[layer][bass.ds(starts[slot], WIN), :]
                                     ).then_inc(window_ready[slot], 16)
                if layer:
                    sp.wait_ge(pre_ready, layer * GROUPS + SLOTS)
                    for ready in src_ready:
                        sp.wait_ge(ready, (part_fills(layer, 0) - 1) * 16)
                for k, ready in enumerate(src_ready):
                    at = slice(k * IX_PART, (k + 1) * IX_PART)
                    sp.dma_start(src_ix[:, at, :].rearrange("p s t -> p (s t)"),
                                 d["src_tiles"][:, at.start * TPG:at.stop * TPG]).then_inc(ready, 16)
                if layer == 0:
                    spread_base()
                in_blocks(sp, body)

            def all_windows(layer):
                if layer == 0:
                    spread_base()
                for q in range(2) if layer == 0 else ():
                    sp.wait_ge(b0_stored[q], 16 * ((WIDES + 1 - q) // 2))
                if layer:
                    sp.wait_ge(b1_stored, CHUNKS * 16)
                with sp.Fori(0, GROUPS) as g:
                    n = g + layer * GROUPS
                    sp.wait_ge(g_added, n * WINDOWS + 1)
                    sp.nop(nofuse=True)
                    sp.dma_start(src_ix[:, 0, :], d["src_tiles"][:, bass.ds(g * TPG, TPG)]).then_inc(g_src_ready, 16)
                    with sp.Fori(0, WINDOWS) as w:
                        sp.wait_ge(g_added, n * WINDOWS + w + 1)
                        sp.nop(nofuse=True)
                        sp.dma_start(window[:, 0, :], b_table[layer][bass.ds(w * WIN, WIN), :]).then_inc(g_window_ready, 16)

            sp.wait_ge(flag_ready, 1)
            many = sp.value_load(flag[0:1, 0:1], min_val=0, max_val=1)
            for layer in range(LAYERS):
                with sp.If(many == 0):
                    few_windows(layer)
                with sp.Else():
                    all_windows(layer)
            sp.wait_ge(y_stored, CHUNKS * 16)

        @block.gpsimd
        def _(pool):
            pool.iota(iota_i[:, :], pattern=[[1, 128]], base=0, channel_multiplier=0).then_inc(iotas_made, 1)
            pool.iota(part_i[:, :], pattern=[[0, 1]], base=0, channel_multiplier=1).then_inc(iotas_made, 1)
            pool.iota(win_i[:, :], pattern=[[WIN, WINDOWS]], base=0, channel_multiplier=0).then_inc(iotas_made, 1)
            pool.memset(acc[:, :], 0.0).then_inc(cleared, 1)
            pool.memset(degree[:, :], 0.0).then_inc(cleared, 1)

            pool.wait_ge(flag_ready, 1)
            many = pool.value_load(flag[0:1, 0:1], min_val=0, max_val=1)

            def gather(layer, slot, t, done):
                pool.indirect_dma_start(
                    out=rows[:, slot, t * FEAT:(t + 1) * FEAT], out_offset=None, in_=a_table[layer][:, :],
                    in_offset=bass.IndirectOffsetOnAxis(ap=src_ix[:, slot, t:t + 1], axis=0)).then_inc(done, 16)

            def few_windows(layer):
                def body(b, n, c):
                    for i in range(n):
                        if i % IX_PART == 0:
                            pool.wait_ge(src_ready[i // IX_PART], part_fills(layer, b) * 16)
                            pool.nop(nofuse=True)
                        pool.wait_ge(pre_ready, b * BLOCK + i + layer * GROUPS + 1)
                        pool.nop(nofuse=True)
                        for t in range(TPG):
                            gather(layer, i, t, rows_ready[i])
                in_blocks(pool, body)

            def all_windows(layer):
                with pool.Fori(0, GROUPS) as g:
                    pool.wait_ge(g_src_ready, (g + layer * GROUPS + 1) * 16)
                    pool.nop(nofuse=True)
                    for t in range(TPG):
                        gather(layer, 0, t, g_rows_ready)

            for layer in range(LAYERS):
                if layer:
                    pool.wait_ge(a1_stored, CHUNKS * 16)
                else:
                    pool.wait_ge(a0_stored, 16 * WIDES)
                    pool.nop(nofuse=True)
                    pool.wait_ge(unfit_found, 1)
                pool.nop(nofuse=True)
                with pool.If(many == 0):
                    few_windows(layer)
                with pool.Else():
                    all_windows(layer)

        @block.tensor
        def _(pe):
            def table(h, w, weights, out):
                for k in range(w // 128):
                    last = nc.tensor.matmul(out[:, k, :], h[:, k * 128:(k + 1) * 128], weights, start=True, stop=True)
                return last

            w_m1a, w_m1b = ([w_m1[:, layer, k * FEAT:(k + 1) * FEAT] for layer in range(LAYERS)] for k in range(2))

            pe.wait_ge(early_in, EARLY_LOADS)
            nc.tensor.matmul(ps[:, 7, 0:FEAT], w_enc_out[:, :], w_m1a[0], start=True, stop=True).then_inc(w_a0_ready, 1)
            pe.wait_ge(b_enc_spread, 1)
            nc.tensor.matmul(ps[:, 6, 0:FEAT], b_enc_all[:, :], w_m1a[0], start=True, stop=True).then_inc(b_bias_ready, 1)

            pe.wait_ge(w_a0_kept, 1)
            for c in range(WIDES):
                if c % X_PART == 0:
                    pe.wait_ge(x_in[c // X_PART], 16)
                if c >= 2:
                    pe.wait_ge(a0_staged, c - 1)
                table(xT[:, c * WIDE:c * WIDE + width(c)], width(c), w_a0[:, :], a0_ps[c % 2]).then_inc(a0_ready, 1)

            pe.wait_ge(unfit_found, 1)
            nc.tensor.matmul(ps[0:1, 7, 0:1], unfit_any[:, :], ones_col[:, :], start=True, stop=True).then_inc(unfit_counted, 1)

            def encode(c, q, w):
                nc.tensor.matmul(enc_ps[q][:, 0:w], w_enc[:, :], wide(xT, c, w), start=True, stop=True).then_inc(enc_ready, 1)

            def stage0(c, q, r, w):
                if not is_last_wide(c):
                    encode(c + 1, 1 - q, width(c + 1))
                pe.wait_ge(h_ready, c + 1)
                if not early(c):
                    pe.wait_ge(b_full_ready, c - 1)
                table(h_new[:, q, :], w, w_m1b[0], b0_ps[q]).then_inc(table_ready, 1)

            pe.wait_ge(late_in, LATE_LOADS)
            encode(0, 0, width(0))
            in_wides(pe, stage0)
            pe.wait_ge(consts_made, 1)
            pe.wait_ge(flag_ready, 1)
            many = pe.value_load(flag[0:1, 0:1], min_val=0, max_val=1)
            pe.wait_ge(b_staged, WIDES)
            pe.wait_ge(a0_staged, WIDES)

            def mean(m, w):
                pe.wait_ge(u_ready, m + 1)
                nc.tensor.matmul(mean_ps[:, 0:w], averager[:, :], u_s[:, 0:w], start=True, stop=True).then_inc(mean_ready, 1)

            def var(m, w):
                pe.wait_ge(sq_ready, m + 1)
                nc.tensor.matmul(var_ps[:, 0:w], averager[:, :], sq[:, 0:w], start=True, stop=True).then_inc(var_ready, 1)

            def step(layer, c, k, w):
                n = c + layer * CHUNKS
                if k == 0:
                    if layer == 0:
                        pe.wait_ge(b_staged, n + WIDES)
                    else:
                        pe.wait_ge(std_ready, norms(layer, c, 0))
                    nc.tensor.matmul(agg_ps[:, 0:w], w_m2[:, layer, :], chunk(acc, c, w), start=True, stop=False)
                    nc.tensor.matmul(agg_ps[:, 0:w], bm2_row[:, layer, :], chunk(degree, c, w), start=False, stop=True
                                     ).then_inc(agg_ready, 1)
                    nc.tensor.matmul(upd_ps[:, 0:w], w_uh[:, layer, :], chunk(hT, c, w), start=True, stop=False)
                elif k == 1:
                    pe.wait_ge(agg_copied, n + 1)
                    nc.tensor.matmul(upd_ps[:, 0:w], w_ua[:, layer, :], agg_s[:, 0:w], start=False, stop=True
                                     ).then_inc(upd_ready, 1)
                elif k == 2:
                    mean(norms(layer, c, 0), w)
                elif k == 3:
                    var(norms(layer, c, 0), w)
                elif k == 5:
                    pe.wait_ge(h_ready, n + WIDES + 1)
                    if layer == 0:
                        table(h_new[:, 0, :], w, w_m1a[1], a1_ps)
                        table(h_new[:, 0, :], w, w_m1b[1], b1_ps).then_inc(table_ready, 1)
                    else:
                        nc.tensor.matmul(agg_ps[:, 0:w], w_out[:, :], h_new[:, 0, 0:w], start=True, stop=True
                                         ).then_inc(proj_ready, 1)
                elif k == 6 and layer == 1:
                    mean(norms(layer, c, 1), w)
                elif k == 7 and layer == 1:
                    var(norms(layer, c, 1), w)

            def flip(o, q, done):
                for t in range(TPG):
                    at = slice(t * 128, (t + 1) * 128)
                    last = nc.tensor.transpose(flipped[:, q, at], onehot[:, o, at], ident[:, :])
                last.then_inc(done, 1)

            def pick(slot, q, done):
                for t in range(TPG):
                    at = slice(t * 128, (t + 1) * 128)
                    for p in range(PARTS):
                        last = nc.tensor.matmul(picked[:, q, at], spread[:, q, at],
                                                window[:, slot, p * FEAT:(p + 1) * FEAT],
                                                start=(p == 0), stop=(p == PARTS - 1))
                last.then_inc(done, 1)

            def count_edges(layer, o, q):
                for t in range(TPG if layer == 0 else 0):
                    at = slice(t * 128, (t + 1) * 128)
                    nc.tensor.matmul(summed_ps[0:1, q, WIN:2 * WIN], ones_col[:, :], onehot[:, o, at],
                                     start=(t == 0), stop=(t == TPG - 1))

            def sum_up(o, q, done):
                for t in range(TPG):
                    at = slice(t * 128, (t + 1) * 128)
                    last = nc.tensor.matmul(summed_ps[:, q, 0:WIN], msg[:, q, at], onehot[:, o, at],
                                            start=(t == 0), stop=(t == TPG - 1))
                last.then_inc(done, 1)

            def few_windows(layer):
                def flip_group(b, i):
                    g = b * BLOCK + i + layer * GROUPS
                    pe.wait_ge(onehot_ready, g + SLOTS + 1)
                    pe.wait_ge(spread_ready, g + SLOTS - 1)
                    flip(i % 4, i % 2, flipped_ready)

                def pick_group(b, i):
                    g = b * BLOCK + i + layer * GROUPS
                    pe.wait_ge(spread_ready, g + SLOTS + 1)
                    pe.wait_ge(window_ready[i % WIN_SLOTS], fills(layer, b, i, WIN_SLOTS) * 16)
                    pe.wait_ge(pre_ready, g + SLOTS - 1)
                    pick(i % WIN_SLOTS, i % 2, picked_ready)

                def body(b, n, c):
                    for i in range(n):
                        g = b * BLOCK + i + layer * GROUPS
                        if there_is(b, i + 1):
                            pick_group(b, i + 1)
                        if there_is(b, i + 2):
                            flip_group(b, i + 2)
                        if c is not None:
                            if i == 0:
                                pe.wait_ge(added, g + SLOTS)
                            for k in steps_beside(i, n):
                                step(layer, c, k, CHUNK)
                        pe.wait_ge(added, g + SLOTS - 1)
                        count_edges(layer, i % 4, i % 2)
                        pe.wait_ge(msg_ready, g + SLOTS + 1)
                        sum_up(i % 4, i % 2, summed_ready)
                flip_group(0, 0)
                pick_group(0, 0)
                if there_is(0, 1):
                    flip_group(0, 1)
                in_blocks(pe, body)
                pe.wait_ge(edges_done, layer + 1)
                in_rest(pe, BESIDE + TAIL, step, layer)

            def all_windows(layer):
                with pe.Fori(0, GROUPS) as g:
                    with pe.Fori(0, WINDOWS) as w:
                        n = (g + layer * GROUPS) * WINDOWS + w
                        pe.wait_ge(g_onehot_ready, n + 1)
                        flip(0, 0, g_flipped_ready)
                        pe.wait_ge(g_spread_ready, n + 1)
                        pe.wait_ge(g_window_ready, n * 16 + 16)
                        pick(0, 0, g_picked_ready)
                        pe.wait_ge(g_msg_ready, n + 1)
                        count_edges(layer, 0, 0)
                        sum_up(0, 0, g_summed_ready)
                pe.wait_ge(edges_done, layer + 1)
                in_rest(pe, 0, step, layer)

            for layer in range(LAYERS):
                with pe.If(many == 0):
                    few_windows(layer)
                with pe.Else():
                    all_windows(layer)

        @block.scalar
        def _(act):
            def b_hi(n, q, w):
                act.wait_ge(b_full_ready, n + 1)
                nc.scalar.activation(b_stage[:, q, 0:w // 128, 0, :], b_full[:, q, 0:w // 128, :], ACT.Copy).then_inc(b_hi_ready, 1)

            def b_mid(n, q, w):
                act.wait_ge(b_rest_ready, n + 1)
                nc.scalar.activation(b_stage[:, q, 0:w // 128, 1, :], b_rest[:, q, 0:w // 128, :], ACT.Copy).then_inc(b_mid_ready, 1)

            def encoded(c, q, w):
                act.wait_ge(enc_ready, c + 1)
                if not early(c):
                    act.wait_ge(h_kept, c - 1)
                nc.scalar.activation(h_new[:, q, 0:w], enc_ps[q][:, 0:w], ACT.Identity, bias=cols[:, 0:1]).then_inc(h_ready, 1)

            def stage0(c, q, r, w):
                if not is_last_wide(c):
                    encoded(c + 1, 1 - q, width(c + 1))
                if not early(c) or c == 1:
                    b_mid(c - 1, 1 - q, WIDE)
                if not early(c):
                    act.wait_ge(b0_stored[q], r * 16)
                b_hi(c, q, w)
                if not early(c) or c == 1:
                    store_b(c - 1, 1 - q, WIDE)

            def store_b(c, q, w):
                act.wait_ge(b_staged, c + 1)
                act.nop(nofuse=True)
                act.dma_start(by_node(b_table[0], c * WIDE, w), b_rows(q, w)).then_inc(b0_stored[q], 16)

            load(act, ("w_enc_out", "cols", "w_m1", "floor"), early_in)
            act.dma_start(bm1_all[:, :, :], d["bm1"].rearrange("(o l) f -> o l f", o=1).broadcast_to([128, LAYERS, FEAT])
                          ).then_inc(early_in, 16)
            act.wait_ge(early_in, EARLY_LOADS)
            for c in range(WIDES):
                act.wait_ge(a0_ready, c + 1)
                nc.scalar.activation(a0_stage[:, c * WIDE // 128:(c * WIDE + width(c)) // 128, :],
                                     a0_ps[c % 2][:, 0:width(c) // 128, :], ACT.Copy).then_inc(a0_staged, 1)
            encoded(0, 0, width(0))
            in_wides(act, stage0)
            b_mid(WIDES - 1, (WIDES - 1) % 2, width(WIDES - 1))
            store_b(WIDES - 1, (WIDES - 1) % 2, width(WIDES - 1))
            act.wait_ge(flag_ready, 1)
            many = act.value_load(flag[0:1, 0:1], min_val=0, max_val=1)
            for q in range(2):
                act.wait_ge(b0_stored[q], 16 * ((WIDES + 1 - q) // 2))

            def square(m, w):
                act.wait_ge(dev_ready, m + 1)
                nc.scalar.activation(sq[:, 0:w], dev[:, 0:w], ACT.Square).then_inc(sq_ready, 1)

            def root(m, w):
                act.wait_ge(var_ready, m + 1)
                nc.scalar.activation(std[:, 0:w], var_ps[:, 0:w], ACT.Sqrt, bias=eps_col[:, :]).then_inc(std_ready, 1)

            def step(layer, c, k, w):
                n = c + layer * CHUNKS
                if k == 0:
                    act.wait_ge(agg_ready, n + 1)
                    nc.scalar.activation(agg_s[:, 0:w], agg_ps[:, 0:w], ACT.Copy).then_inc(agg_copied, 1)
                elif k == 2:
                    square(norms(layer, c, 0), w)
                elif k == 3:
                    root(norms(layer, c, 0), w)
                elif k == 5 and layer == 0:
                    act.wait_ge(table_ready, n + WIDES + 1)
                    nc.scalar.activation(a_rows(w), a1_ps[:, 0:w // 128, :], ACT.Copy).then_inc(a_staged, 1)
                    act.wait_ge(a_staged, n + 1)
                    act.dma_start(by_node(a_table[1], c * CHUNK, w), a_rows(w)).then_inc(a1_stored, 16)
                elif k == 6 and layer == 0:
                    b_hi(n + WIDES, 0, w)
                    nc.scalar.activation(chunk(hT, c, w), h_new[:, 0, 0:w], ACT.Copy).then_inc(h_kept, 1)
                elif k == 7 and layer == 0:
                    b_mid(n + WIDES, 0, w)
                elif k == 9 and layer == 0:
                    act.wait_ge(b_staged, n + WIDES + 1)
                    act.dma_start(by_node(b_table[1], c * CHUNK, w), b_rows(0, w)).then_inc(b1_stored, 16)
                elif k == 12 and layer == 0:
                    act.wait_ge(a1_stored, (c + 1) * 16)
                    act.wait_ge(b1_stored, (c + 1) * 16)
                elif k == 6:
                    square(norms(layer, c, 1), w)
                elif k == 7:
                    root(norms(layer, c, 1), w)
                elif k == 9:
                    act.wait_ge(out_ready, c + 1)
                    act.dma_start(d["yT"][:, bass.ds(c * CHUNK, w)], y_out[:, 0:w]).then_inc(y_stored, 16)
                elif k == 12:
                    act.wait_ge(y_stored, (c + 1) * 16)

            def few_windows(layer):
                def spread_group(b, i):
                    g, q = b * BLOCK + i + layer * GROUPS, i % 2
                    act.wait_ge(flipped_ready, g + SLOTS + 1)
                    act.wait_ge(picked_ready, g + SLOTS - 1)
                    nc.scalar.activation(spread[:, q, :], flipped[:, q, :], ACT.Copy).then_inc(spread_ready, 1)

                def body(b, n, c):
                    for i in range(n):
                        g, q = b * BLOCK + i + layer * GROUPS, i % 2
                        act.wait_ge(pre_ready, g + SLOTS + 1)
                        act.wait_ge(summed_ready, g + SLOTS - 1)
                        nc.scalar.activation(msg[:, q, :], pre[:, q, :], ACT.Relu).then_inc(msg_ready, 1)
                        if there_is(b, i + 2):
                            spread_group(b, i + 2)
                        if refills(b, i):
                            at = bass.ds(((b + 1) * BLOCK + i + 1 - IX_PART) * TPG, IX_PART * TPG)
                            act.dma_start(src_ix[:, i + 1 - IX_PART:i + 1, :].rearrange("p s t -> p (s t)"),
                                          d["src_tiles"][:, at]).then_inc(src_ready[i // IX_PART], 16)
                        if c is not None:
                            for k in steps_beside(i, n):
                                step(layer, c, k, CHUNK)
                spread_group(0, 0)
                if there_is(0, 1):
                    spread_group(0, 1)
                in_blocks(act, body)
                in_rest(act, BESIDE + TAIL, step, layer)

            def all_windows(layer):
                with act.Fori(0, GROUPS) as g:
                    with act.Fori(0, WINDOWS) as w:
                        n = (g + layer * GROUPS) * WINDOWS + w
                        act.wait_ge(g_flipped_ready, n + 1)
                        nc.scalar.activation(spread[:, 0, :], flipped[:, 0, :], ACT.Copy).then_inc(g_spread_ready, 1)
                        act.wait_ge(g_pre_ready, n + 1)
                        nc.scalar.activation(msg[:, 0, :], pre[:, 0, :], ACT.Relu).then_inc(g_msg_ready, 1)
                in_rest(act, 0, step, layer)

            for layer in range(LAYERS):
                with act.If(many == 0):
                    few_windows(layer)
                with act.Else():
                    all_windows(layer)

        @block.vector
        def _(dve):
            steps = [0]

            def link(ins):
                steps[0] += 1
                ins.then_inc(dve_step, 1)
                dve.wait_ge(dve_step, steps[0])

            for ring in (onehot_ready, flipped_ready, spread_ready, picked_ready, pre_ready, msg_ready,
                         summed_ready, added):
                dve.sem_inc(ring, SLOTS)
            dve.sem_inc(g_added, 1)

            nc.vector.memset(ones_col[:, :], 1.0)
            nc.vector.memset(averager[:, :], 1.0 / FEAT)
            nc.vector.memset(eps_col[:, :], EPS)
            nc.vector.memset(zeros[:, :], 0.0)
            dve.wait_ge(iotas_made, 3)
            nc.vector.tensor_copy(iota[:, :], iota_i[:, :])
            nc.vector.tensor_copy(win_start[:, :], win_i[:, :])
            link(nc.vector.tensor_copy(part[:, :], part_i[:, :]))
            nc.vector.tensor_scalar(ident[:, :], iota[:, :], part[:, 0:1], None, ALU.is_equal).then_inc(consts_made, 1)

            dve.wait_ge(early_in, EARLY_LOADS)
            nc.vector.tensor_copy(b_enc_all[:, :], cols[:, 0:1].broadcast_to([FEAT, 128])).then_inc(b_enc_spread, 1)
            dve.wait_ge(w_a0_ready, 1)
            nc.vector.tensor_copy(w_a0[:, :], ps[:, 7, 0:FEAT]).then_inc(w_a0_kept, 1)
            dve.wait_ge(b_bias_ready, 1)
            nc.vector.tensor_tensor(bm1_all[:, 0, :], bm1_all[:, 0, :], ps[:, 6, 0:FEAT], ALU.add).then_inc(b_bias_kept, 1)

            dve.wait_ge(dst_g_in, 16)
            link(nc.vector.tensor_copy(dst_gf, dst_g))
            by_group = lambda buf: buf.rearrange("p (k e) -> p k e", e=GROUP)
            nc.vector.tensor_reduce(gmin[:, :], by_group(dst_gf), AX.X, ALU.min)
            link(nc.vector.scalar_tensor_tensor(dst_gv, dst_gf, float(NO_NODE), dst_gf, ALU.is_lt, ALU.mult))
            nc.vector.tensor_reduce(gmax[:, :], by_group(dst_gv), AX.X, ALU.max)
            nc.vector.tensor_scalar(base[:, :], gmin[:, :], float(TOP), 0.0, ALU.min, ALU.max).then_inc(base_found, 1)
            dve.wait_ge(base_found, 1)
            nc.vector.tensor_tensor(unfit[:, 1, :], floor[:, :], base[:, :], ALU.is_gt)
            link(nc.vector.tensor_tensor(spans[:, :], gmax[:, :], base[:, :], ALU.subtract))
            link(nc.vector.tensor_scalar(unfit[:, 0, :], spans[:, :], float(WIN), None, ALU.is_ge))
            nc.vector.tensor_reduce(unfit_any[:, :], unfit[:, :, :], AX.XY, ALU.max).then_inc(unfit_found, 1)

            def b_full_step(stage, n, q, w, b_out):
                dve.wait_ge(table_ready, n + 1)
                nc.vector.tensor_tensor(b_full[:, q, 0:w // 128, :], b_out[:, 0:w // 128, :],
                                        bm1_all[:, stage:stage + 1, :].broadcast_to([128, w // 128, FEAT]),
                                        ALU.add).then_inc(b_full_ready, 1)

            def b_rest_step(n, q, w):
                dve.wait_ge(b_hi_ready, n + 1)
                nc.vector.tensor_tensor(b_rest[:, q, 0:w // 128, :], b_full[:, q, 0:w // 128, :],
                                        b_stage[:, q, 0:w // 128, 0, :], ALU.subtract).then_inc(b_rest_ready, 1)

            def b_lo_step(n, q, w):
                dve.wait_ge(b_mid_ready, n + 1)
                nc.vector.tensor_tensor(b_stage[:, q, 0:w // 128, 2, :], b_rest[:, q, 0:w // 128, :],
                                        b_stage[:, q, 0:w // 128, 1, :], ALU.subtract).then_inc(b_staged, 1)

            def relate():
                dve.wait_ge(base_spread, 16)
                nc.vector.tensor_copy(base_row[:, :], base_all[0:1, :]).then_inc(rows_of_base, 1)
                dve.wait_ge(rows_of_base, 1)
                dve.wait_ge(dst_in, 16)
                link(nc.vector.tensor_copy(dst_f[:, :], dst_i[:, :]))
                nc.vector.tensor_tensor(rel.rearrange("p (g t) -> p g t", t=TPG),
                                        dst_f[:, :].rearrange("p (g t) -> p g t", t=TPG),
                                        base_all[:, 0:GROUPS].rearrange("p (g o) -> p g o", o=1).broadcast_to([128, GROUPS, TPG]),
                                        ALU.subtract).then_inc(rel_ready, 1)

            def stage0(c, q, r, w):
                if isinstance(c, int) and c == max(0, WIDES - 2):
                    relate()
                dve.wait_ge(h_ready, c + 1)
                nc.vector.tensor_copy(wide(hT, c, w), h_new[:, q, 0:w]).then_inc(h_kept, 1)
                b_full_step(0, c, q, w, b0_ps[q])
                if not early(c) or c == 1:
                    b_lo_step(c - 1, 1 - q, WIDE)
                b_rest_step(c, q, w)

            dve.wait_ge(unfit_counted, 1)
            nc.vector.tensor_scalar(flag[:, :], ps[0:1, 7, 0:1], 0.0, None, ALU.is_gt).then_inc(flag_ready, 1)
            dve.wait_ge(a0_stored, 16 * WIDES)
            dve.wait_ge(b_bias_kept, 1)
            in_wides(dve, stage0)
            b_lo_step(WIDES - 1, (WIDES - 1) % 2, width(WIDES - 1))

            dve.wait_ge(flag_ready, 1)
            many = dve.value_load(flag[0:1, 0:1], min_val=0, max_val=1)
            dve.wait_ge(rel_ready, 1)
            dve.wait_ge(cleared, 2)

            def deviation(m, w):
                dve.wait_ge(mean_ready, m + 1)
                nc.vector.tensor_tensor(dev[:, 0:w], u_s[:, 0:w], mean_ps[:, 0:w], ALU.subtract).then_inc(dev_ready, 1)

            def inverse(m, w):
                dve.wait_ge(std_ready, m + 1)
                nc.vector.reciprocal(rstd[:, 0:w], std[:, 0:w]).then_inc(rstd_ready, 1)
                dve.wait_ge(rstd_ready, m + 1)

            def step(layer, c, k, w):
                n = c + layer * CHUNKS
                bu, gamma, beta = (cols[:, 2 + 3 * layer + j:3 + 3 * layer + j] for j in range(3))
                if k == 1:
                    dve.wait_ge(upd_ready, n + 1)
                    nc.vector.scalar_tensor_tensor(u_s[:, 0:w], upd_ps[:, 0:w], bu, chunk(hT, c, w), ALU.add, ALU.add
                                                   ).then_inc(u_ready, 1)
                    if layer + 1 < LAYERS:
                        nc.vector.tensor_copy(chunk(acc, c, w), zeros[:, 0:w]).then_inc(acc_cleared, 1)
                elif k == 2:
                    deviation(norms(layer, c, 0), w)
                elif k == 4:
                    inverse(norms(layer, c, 0), w)
                    nc.vector.tensor_tensor(rstd[:, 0:w], rstd[:, 0:w], dev[:, 0:w], ALU.mult).then_inc(norm_ready, 1)
                    dve.wait_ge(h_kept, c + WIDES if layer == 0 else CHUNKS + WIDES)
                    dve.wait_ge(norm_ready, n + 1)
                    nc.vector.tensor_scalar(h_new[:, 0, 0:w], rstd[:, 0:w], gamma, beta, ALU.mult, ALU.add
                                            ).then_inc(h_ready, 1)
                elif k == 5 and layer == 0:
                    b_full_step(1, n + WIDES, 0, w, b1_ps)
                elif k == 7 and layer == 0:
                    b_rest_step(n + WIDES, 0, w)
                elif k == 8 and layer == 0:
                    b_lo_step(n + WIDES, 0, w)
                elif k == 5:
                    dve.wait_ge(proj_ready, c + 1)
                    nc.vector.scalar_tensor_tensor(u_s[:, 0:w], agg_ps[:, 0:w], cols[:, 1:2], chunk(xT, c, w), ALU.add, ALU.add
                                                   ).then_inc(u_ready, 1)
                elif k == 6 and layer == 1:
                    deviation(norms(layer, c, 1), w)
                elif k == 8:
                    inverse(norms(layer, c, 1), w)
                    nc.vector.tensor_tensor(y_out[:, 0:w], rstd[:, 0:w], dev[:, 0:w], ALU.mult).then_inc(out_ready, 1)

            def one_hots(rel_cols, q):
                return nc.vector.tensor_tensor(
                    onehot[:, q, :].rearrange("p (t n) -> p t n", t=TPG),
                    iota[:, :].rearrange("p (o n) -> p o n", o=1).broadcast_to([TILE, TPG, WIN]),
                    rel_cols.rearrange("p (t o) -> p t o", o=1).broadcast_to([TILE, TPG, WIN]), ALU.is_equal)

            def add_sums(layer, start, q, done):
                at = bass.ds(start, WIN)
                last = nc.vector.tensor_tensor(acc[:, at], acc[:, at], summed_ps[:, q, 0:WIN], ALU.add)
                if layer == 0:
                    last = nc.vector.tensor_tensor(degree[:, at], degree[:, at], summed_ps[0:1, q, WIN:2 * WIN], ALU.add)
                last.then_inc(done, 1)

            def few_windows(layer):
                def onehot_group(b, i):
                    g = b * BLOCK + i
                    dve.wait_ge(summed_ready, g + layer * GROUPS + SLOTS - 3)
                    one_hots(rel[:, bass.ds(g * TPG, TPG)], i % 4).then_inc(onehot_ready, 1)

                def pre_group(b, i):
                    g, q, slot = b * BLOCK + i + layer * GROUPS, i % 2, i % SLOTS
                    dve.wait_ge(rows_ready[slot], fills(layer, b, i, SLOTS) * (16 * TPG))
                    dve.wait_ge(picked_ready, g + SLOTS + 1)
                    dve.wait_ge(msg_ready, g + SLOTS - 1)
                    nc.vector.tensor_tensor(pre[:, q, :], rows[:, slot, :], picked[:, q, :], ALU.add).then_inc(pre_ready, 1)

                def body(b, n, c):
                    for i in range(n):
                        g = b * BLOCK + i + layer * GROUPS
                        if i % WIN_SLOTS == 0:
                            starts = load_starts(mybir.EngineType.DVE, b, i, n)
                        if there_is(b, i + 2):
                            onehot_group(b, i + 2)
                        if there_is(b, i + 1):
                            pre_group(b, i + 1)
                        if c is not None:
                            for k in steps_beside(i, n):
                                step(layer, c, k, CHUNK)
                        dve.wait_ge(summed_ready, g + SLOTS + 1)
                        dve.wait_ge(added, g + SLOTS)
                        add_sums(layer, starts[i % WIN_SLOTS], i % 2, added)
                onehot_group(0, 0)
                if there_is(0, 1):
                    onehot_group(0, 1)
                pre_group(0, 0)
                in_blocks(dve, body)
                dve.wait_ge(added, (layer + 1) * GROUPS + SLOTS)
                dve.sem_inc(edges_done, 1)
                in_rest(dve, BESIDE + TAIL, step, layer)

            def all_windows(layer):
                with dve.Fori(0, GROUPS) as g:
                    with dve.Fori(0, WINDOWS) as w:
                        n = (g + layer * GROUPS) * WINDOWS + w
                        nc.vector.tensor_scalar(rel_win[:, :], dst_f[:, bass.ds(g * TPG, TPG)],
                                                win_start[:, bass.ds(w, 1)], None, ALU.subtract).then_inc(g_rel_ready, 1)
                        dve.wait_ge(g_rel_ready, n + 1)
                        one_hots(rel_win[:, :], 0).then_inc(g_onehot_ready, 1)
                        dve.wait_ge(g_rows_ready, (g + layer * GROUPS + 1) * (16 * TPG))
                        dve.wait_ge(g_picked_ready, n + 1)
                        nc.vector.tensor_tensor(pre[:, 0, :], rows[:, 0, :], picked[:, 0, :], ALU.add
                                                ).then_inc(g_pre_ready, 1)
                        dve.wait_ge(g_summed_ready, n + 1)
                        add_sums(layer, w * WIN, 0, g_added)
                        dve.wait_ge(g_added, n + 2)
                dve.sem_inc(edges_done, 1)
                in_rest(dve, 0, step, layer)

            for layer in range(LAYERS):
                if layer:
                    dve.wait_ge(acc_cleared, CHUNKS)
                with dve.If(many == 0):
                    few_windows(layer)
                with dve.Else():
                    all_windows(layer)


def kernel(**inputs):
    import numpy as _np
    import concourse.bacc as _bacc
    from concourse import mybir as _mybir
    from concourse.bass_utils import run_bass_kernel_spmd as _run

    a = {k.removeprefix("L0_gnn_"): _np.asarray(v) for k, v in inputs.items()}
    nodes, edges = a["x"].shape[0], a["src"].shape[0]
    groups, npad, per_row, _, _, _, beside, tail = sizes(nodes, edges)

    def turned(w):
        return _np.ascontiguousarray(_np.swapaxes(w, -1, -2))

    def by_input(w):
        return _np.ascontiguousarray(_np.swapaxes(w, 0, 1))

    xT = _np.zeros((FEAT, npad), a["x"].dtype)
    xT[:, :nodes] = a["x"].T
    src_groups = ((groups - 1) // BLOCK + 1) * BLOCK
    src = _np.zeros(src_groups * GROUP, a["src"].dtype)
    src[:edges] = a["src"]
    dst = _np.full(128 * per_row * GROUP, NO_NODE, a["dst"].dtype)
    dst[:edges] = a["dst"]
    begun = _np.clip(_np.arange(128 * per_row) // BLOCK - LEAD + 1, 0, beside + tail)
    m1 = turned(a["Wm1"])
    u = turned(a["Wu"])
    per_layer = [a[k][l] for l in range(LAYERS) for k in ("bu", "gamma", "beta")]
    arrays = {
        "xT": xT,
        "src_tiles": _np.ascontiguousarray(src.reshape(src_groups * TPG, TILE).T),
        "dst_tiles": _np.ascontiguousarray(dst[:groups * GROUP].reshape(groups * TPG, TILE).T),
        "dst_groups": dst.reshape(128, per_row * GROUP),
        "w_enc": turned(a["W_enc"]),
        "w_enc_out": a["W_enc"],
        "w_out": turned(a["W_out"]),
        "w_m1": by_input(_np.concatenate([m1[:, :FEAT], m1[:, FEAT:]], axis=2)),
        "w_m2": by_input(turned(a["Wm2"])),
        "w_uh": by_input(u[:, :FEAT]),
        "w_ua": by_input(u[:, FEAT:]),
        "cols": _np.ascontiguousarray(_np.stack([a["b_enc"], a["b_out"], *per_layer], axis=1)),
        "floor": (begun * CHUNK).astype(_np.float32).reshape(128, per_row),
        "bm1": a["bm1"],
        "bm2_row": a["bm2"].reshape(1, LAYERS, FEAT),
    }
    nc = _bacc.Bacc("TRN2", target_bir_lowering=False, num_devices=1)
    d = {k: nc.dram_tensor("in_" + k, v.shape, _mybir.dt.from_np(v.dtype), kind="ExternalInput").ap() for k, v in arrays.items()}
    d["yT"] = nc.dram_tensor("yT", (FEAT, npad), _mybir.dt.float32, kind="ExternalOutput").ap()
    build(nc, d, nodes, edges)
    r = _run(nc, [{"in_" + k: v for k, v in arrays.items()}], core_ids=[0])
    return _np.ascontiguousarray(r.results[0]["yT"][:, :nodes].T)
```
